# Optimizing a Trainium2 kernel written in Bass

```python
import numpy as np
import jax
import jax.numpy as jnp

def _softmax(x, axis=-1):
    return jax.nn.softmax(x, axis=axis)

def _gelu(x):
    return jax.nn.gelu(x, approximate=True)

def _silu(x):
    return jax.nn.silu(x)

def _sigmoid(x):
    return jax.nn.sigmoid(x)

def _layernorm(x, axis=-1, eps=1e-05):
    m = jnp.mean(x, axis=axis, keepdims=True)
    v = jnp.var(x, axis=axis, keepdims=True)
    return (x - m) / jnp.sqrt(v + eps)

def _scatter_add(tgt, idx, src, axis=0):
    return tgt.at[idx].add(src)

def _segment_sum(src, seg, n):
    return jax.ops.segment_sum(src, seg, n)
kernel_name = 'mk_xattn_ffn_d1_seqx_r8_ee8f6a'

def setup_inputs(seed: int=0):
    np.random.seed(seed)
    _w = jnp.asarray

    def _rec_inputs():
        import jax
        import jax.numpy as jnp
        _rk = jax.random.key(seed)
        x = -0.0002928 + 1 * jax.random.normal(jax.random.fold_in(_rk, 1), (4, 256, 128), jnp.float32)
        _lenS = 256 - jax.random.randint(jax.random.fold_in(_rk, 7), (4,), 0, max(1, 256 // 4) + 1, jnp.int32)
        _lenS2 = 256 - jax.random.randint(jax.random.fold_in(_rk, 8), (4,), 0, max(1, 256 // 4) + 1, jnp.int32)
        _ctx_1024P = jax.random.normal(jax.random.fold_in(_rk, 11), (4, 16, 128), jnp.float32)
        _ctx_1024c = jax.random.dirichlet(jax.random.fold_in(_rk, 511), 0.3 * jnp.ones((16,), jnp.float32), (4, 256))
        _ctx_1024t = jnp.einsum('bsk,bkd->bsd', _ctx_1024c, _ctx_1024P)
        _ctx_1024t = _ctx_1024t * jax.lax.rsqrt(jnp.mean(jnp.square(_ctx_1024t)) + 1e-12) * 0.953939
        ctx_1024 = -1.39393e-06 + 0.999914 * (_ctx_1024t + 0.3 * jax.random.normal(jax.random.fold_in(_rk, 611), (4, 256, 128), jnp.float32))
        return (x, ctx_1024)
    x, ctx_1024 = _rec_inputs()

    def _L0_xattn_setup():
        import jax, jax.numpy as jnp
        import numpy as np
        import math
        D_MODEL = 128
        NUM_HEADS = 16
        MAX_LEN = 256
        D_HEAD = D_MODEL // NUM_HEADS
        BATCH = 2
        SEQ = 256

        def _skew(QEr):
            B, H, R, C = QEr.shape
            padded = jnp.pad(QEr, ((0, 0), (0, 0), (0, 0), (1, 0)))
            reshaped = padded.reshape(B, H, C + 1, R)
            return reshaped[:, :, 1:, :]
        root = jax.random.key(seed)
        ks = jax.random.split(root, 10)
        s = 1.0 / math.sqrt(D_MODEL)
        return {'query': jax.random.normal(ks[0], (BATCH, SEQ, D_MODEL), jnp.float32), 'key': jax.random.normal(ks[1], (BATCH, SEQ, D_MODEL), jnp.float32), 'value': jax.random.normal(ks[2], (BATCH, SEQ, D_MODEL), jnp.float32), 'Wq': jax.random.normal(ks[3], (D_MODEL, D_MODEL), jnp.float32) * s, 'bq': jax.random.normal(ks[4], (D_MODEL,), jnp.float32) * s, 'Wk': jax.random.normal(ks[5], (D_MODEL, D_MODEL), jnp.float32) * s, 'bk': jax.random.normal(ks[6], (D_MODEL,), jnp.float32) * s, 'Wv': jax.random.normal(ks[7], (D_MODEL, D_MODEL), jnp.float32) * s, 'bv': jax.random.normal(ks[8], (D_MODEL,), jnp.float32) * s, 'Er': jax.random.normal(ks[9], (MAX_LEN, D_HEAD), jnp.float32)}
    _L0_xattn_all = _L0_xattn_setup()
    _L0_xattn_in = {k: v for k, v in _L0_xattn_all.items() if k in ('Wq', 'bq', 'Wk', 'bk', 'Wv', 'bv', 'Er')}
    del _L0_xattn_all

    def _L0_ffn_setup():
        import jax, jax.numpy as jnp
        import numpy as np
        B, T, D, H, E = (4, 256, 128, 256, 8)
        TOP_K = int(E * 0.25)
        key = jax.random.key(seed)
        ks = jax.random.split(key, 6)
        x = jax.random.normal(ks[0], (B, T, D), dtype=jnp.float32)
        gate = jax.random.normal(ks[1], (D, E), dtype=jnp.float32)
        W1 = jax.random.normal(ks[2], (E, D, H), dtype=jnp.float32) * D ** (-0.5)
        b1 = jnp.zeros((E, H), dtype=jnp.float32)
        W2 = jax.random.normal(ks[3], (E, H, D), dtype=jnp.float32) * H ** (-0.5)
        b2 = jnp.zeros((E, D), dtype=jnp.float32)
        return {'x': x, 'gate': gate, 'W1': W1, 'b1': b1, 'W2': W2, 'b2': b2}
    _L0_ffn_all = _L0_ffn_setup()
    _L0_ffn_in = {k: v for k, v in _L0_ffn_all.items() if k in ('gate', 'W1', 'b1', 'W2', 'b2')}
    del _L0_ffn_all
    return {'x': x, 'ctx_1024': ctx_1024, 'L0_xattn_Wq': _L0_xattn_in['Wq'], 'L0_xattn_bq': _L0_xattn_in['bq'], 'L0_xattn_Wk': _L0_xattn_in['Wk'], 'L0_xattn_bk': _L0_xattn_in['bk'], 'L0_xattn_Wv': _L0_xattn_in['Wv'], 'L0_xattn_bv': _L0_xattn_in['bv'], 'L0_xattn_Er': _L0_xattn_in['Er'], 'L0_ffn_gate': _L0_ffn_in['gate'], 'L0_ffn_W1': _L0_ffn_in['W1'], 'L0_ffn_b1': _L0_ffn_in['b1'], 'L0_ffn_W2': _L0_ffn_in['W2'], 'L0_ffn_b2': _L0_ffn_in['b2']}

def reference(x, ctx_1024, L0_xattn_Wq, L0_xattn_bq, L0_xattn_Wk, L0_xattn_bk, L0_xattn_Wv, L0_xattn_bv, L0_xattn_Er, L0_ffn_gate, L0_ffn_W1, L0_ffn_b1, L0_ffn_W2, L0_ffn_b2):
    import jax
    import jax.numpy as jnp

    def _L0_xattn_ref(query, key, value, Wq, bq, Wk, bk, Wv, bv, Er):
        import jax, jax.numpy as jnp
        import numpy as np
        import math
        D_MODEL = 128
        NUM_HEADS = 16
        MAX_LEN = 256
        D_HEAD = D_MODEL // NUM_HEADS
        BATCH = 2
        SEQ = 256

        def _skew(QEr):
            B, H, R, C = QEr.shape
            padded = jnp.pad(QEr, ((0, 0), (0, 0), (0, 0), (1, 0)))
            reshaped = padded.reshape(B, H, C + 1, R)
            return reshaped[:, :, 1:, :]
        B, S, D = query.shape
        H, dh = (NUM_HEADS, D_HEAD)
        q = (jnp.einsum('bsd,ed->bse', query, Wq) + bq).reshape(B, S, H, dh).transpose(0, 2, 1, 3)
        k = (jnp.einsum('bsd,ed->bse', key, Wk) + bk).reshape(B, S, H, dh).transpose(0, 2, 1, 3)
        v = (jnp.einsum('bsd,ed->bse', value, Wv) + bv).reshape(B, S, H, dh).transpose(0, 2, 1, 3)
        start = MAX_LEN - S
        Er_s = Er[start:, :]
        QEr = jnp.einsum('bhsd,ld->bhsl', q, Er_s)
        Srel = _skew(QEr)
        QK = jnp.einsum('bhsd,bhtd->bhst', q, k)
        attn = (QK + Srel) / math.sqrt(dh)
        causal = jnp.tril(jnp.ones((S, S), dtype=bool))
        attn = jnp.where(causal[None, None], attn, -jnp.inf)
        attn = jax.nn.softmax(attn, axis=-1)
        out = jnp.einsum('bhst,bhtd->bhsd', attn, v)
        out = out.transpose(0, 2, 1, 3).reshape(B, S, D)
        return out

    def _L0_ffn_ref(x, gate, W1, b1, W2, b2):
        import jax, jax.numpy as jnp
        import numpy as np
        B, T, D, H, E = (4, 256, 128, 256, 8)
        TOP_K = int(E * 0.25)
        raw_gate = jax.nn.softmax(jnp.einsum('btd,de->bte', x, gate), axis=-1)
        topk_scores, topk_idx = jax.lax.top_k(raw_gate, TOP_K)
        mask = jax.nn.one_hot(topk_idx, E, dtype=raw_gate.dtype).sum(axis=-2)
        gate_topk = mask * raw_gate
        gate_topk = gate_topk / jnp.maximum(gate_topk.sum(axis=-1, keepdims=True), 1e-12)
        h = jax.nn.relu(jnp.einsum('btd,edh->beth', x, W1) + b1[None, :, None, :])
        expert_out = jnp.einsum('beth,ehd->betd', h, W2) + b2[None, :, None, :]
        out = jnp.einsum('bte,betd->btd', gate_topk, expert_out)
        return out
    x = x + _L0_xattn_ref(_layernorm(x, axis=-1), ctx_1024, ctx_1024, L0_xattn_Wq, L0_xattn_bq, L0_xattn_Wk, L0_xattn_bk, L0_xattn_Wv, L0_xattn_bv, L0_xattn_Er)
    x = x + _L0_ffn_ref(_layernorm(x, axis=-1), L0_ffn_gate, L0_ffn_W1, L0_ffn_b1, L0_ffn_W2, L0_ffn_b2)
    return x

_drawn_inputs = setup_inputs


def setup_inputs(seed=0):
    import zlib

    import numpy as np

    out = dict(_drawn_inputs(seed))
    spreads = {'L0_ffn_b1': (0.0, 0.1), 'L0_ffn_b2': (0.0, 0.1)}
    factors = {}
    for name, (base, spread) in spreads.items():
        noise = np.random.default_rng([zlib.crc32(name.encode()), seed]).standard_normal(out[name].shape)
        drawn = base * np.exp(spread * noise) if base else spread * noise
        out[name] = jnp.asarray(drawn.astype(out[name].dtype))
    for name, factor in factors.items():
        out[name] = (out[name] * factor).astype(out[name].dtype)
    return out
```

```python
from contextlib import ExitStack

import numpy as np

import concourse.bass as bass
from concourse import mybir

F32 = mybir.dt.float32
BF16 = mybir.dt.bfloat16
ALU = mybir.AluOpType
ACT = mybir.ActivationFunctionType
AX = mybir.AxisListType

B, S, D, H, DH = 4, 256, 128, 16, 8
E, HID = 8, 256
P = 128
TILES = B * S // P
ROWS = 8
GROUPS = 4
BLOCK = ROWS * GROUPS
BLOCKS = B * S // BLOCK
PER_BATCH = S // BLOCK
PER_TILE = P // BLOCK
PAIRS = 2
BLOCKS_PAIR = BLOCKS // PAIRS
TILES_PAIR = TILES // PAIRS
CHUNKS = 2 * E
MASKED = -1e30
EPS = 1e-5
SCALE = float(DH) ** -0.5
TIE = 1.2e-38
HT_BUFS = 6


def shape_constants():
    part = np.arange(P)
    row_mask = (part[:, None] % ROWS == np.arange(ROWS)).astype(np.float32)
    head_mask = (part[:, None] // DH == np.arange(H)).astype(np.float32)
    col_row = np.tile(np.arange(ROWS), H)
    mask_rows = (np.arange(ROWS)[:, None] == col_row).astype(np.float32)
    mask_keys = np.where(np.arange(BLOCK)[None, :] > np.arange(ROWS)[:, None], MASKED, 0.0).astype(np.float32)
    i, j = np.meshgrid(np.arange(E), np.arange(E), indexing="ij")
    tie = np.broadcast_to(np.where(j < i, TIE, 0.0).astype(np.float32).reshape(1, E * E), (P, E * E))
    wide = np.concatenate([np.eye(P, dtype=np.float32), row_mask, head_mask, tie], axis=1)
    return {"const_wide": np.ascontiguousarray(wide),
            "const_mask": np.ascontiguousarray(np.concatenate([mask_rows, mask_keys], axis=1))}


def units_of(n):
    keys = BLOCK * (n % PER_BATCH + 1)
    return [(c, c * P, min(P, keys - c * P)) for c in range((keys + P - 1) // P)]


UNITS_BEFORE = [0]
for _n in range(BLOCKS):
    UNITS_BEFORE.append(UNITS_BEFORE[-1] + len(units_of(_n)))

LN_T, KV, Q, Q_T, ROWS_0, ROWS_1, ROWS_2, ROWS_3 = range(8)
LN2_T, GATE, GATE_T, BIAS2 = range(4)


def build(nc, t):
    ctx = ExitStack()
    with ctx:
        def sb(name, shape, dt=F32):
            return ctx.enter_context(nc.sbuf_tensor(name, shape, dt))

        def ps(name, shape, dt=F32):
            return ctx.enter_context(nc.psum_tensor(name, shape, dt))

        def sem(name):
            return ctx.enter_context(nc.semaphore(name))

        x_sb = sb("x_sb", [P, TILES, D])
        ctxT = sb("ctxT", [D, B * S])
        wqT = sb("wqT", [D, D])
        wkT = sb("wkT", [D, D])
        wvT = sb("wvT", [D, D])
        bq_row = sb("bq_row", [1, D])
        bv_row = sb("bv_row", [1, D])
        bk_col = sb("bk_col", [D, 1])
        ones_row = sb("ones_row", [1, P])
        er_shift = sb("er_shift", [ROWS * DH, S + ROWS])
        wide = sb("wide", [P, P + ROWS + H + E * E])
        ident = wide[:, 0:P]
        row_mask = wide[:, P:P + ROWS]
        head_mask = wide[:, P + ROWS:P + ROWS + H]
        tie_tri = wide[:, P + ROWS + H:].rearrange("p (i j) -> p i j", i=E)
        mask_f32 = sb("mask_f32", [ROWS, P + BLOCK])
        mask_b16 = sb("mask_b16", [ROWS, P + BLOCK], BF16)
        mask_rows = mask_b16[:, 0:P]
        mask_keys = mask_b16[:, P:P + BLOCK]
        w1 = sb("w1", [D, E, HID])
        w2 = sb("w2", [P, CHUNKS, D])
        b1_col = sb("b1_col", [P, CHUNKS])
        b2_sb = sb("b2_sb", [E, D])
        gate_sb = sb("gate_sb", [D, E])

        stats = sb("stats", [P, TILES, 6])
        mean_var = sb("mean_var", [P, TILES, 2])
        var_eps = sb("var_eps", [P, TILES])
        rstd = sb("rstd", [P, TILES])
        minus_half = sb("minus_half", [P, TILES])
        xn = sb("xn", [P, TILES, D])
        xnT = sb("xnT", [D, S])
        kT = sb("kT", [D, B, S])
        v_one = sb("v_one", [P, TILES, H, DH + 1])
        q_sb = sb("q_sb", [P, 2, D])
        qT = sb("qT", [D, 2, P])
        q_expand = sb("q_expand", [P, 2, H, ROWS * DH])
        q_rows = sb("q_rows", [ROWS * DH, 2, 2, P // ROWS, H, ROWS])
        q_heads = sb("q_heads", [D, 2, 2, P // ROWS, H, ROWS])
        neg_max = sb("neg_max", [P, 4, GROUPS])
        probs = sb("probs", [P, 3, GROUPS, S])
        probsT = sb("probsT", [P, 3, H, P])
        inv_sum = sb("inv_sum", [P, H])
        attn = sb("attn", [P, H, DH])
        x1 = sb("x1", [P, TILES, D])
        stats2 = sb("stats2", [P, 6])
        mean_var2 = sb("mean_var2", [P, 2])
        var_eps2 = sb("var_eps2", [P, 1])
        rstd2 = sb("rstd2", [P, 1])
        xn2 = sb("xn2", [P, D])
        xn2T = sb("xn2T", [D, TILES_PAIR, P])
        logits = sb("logits", [P, E])
        sorted8 = sb("sorted8", [P, E])
        neg_top = sb("neg_top", [P, 1])
        gate_exp = sb("gate_exp", [P, E])
        gate_sum = sb("gate_sum", [P, 1])
        diff = sb("diff", [P, E, E])
        above = sb("above", [P, E, E])
        rank = sb("rank", [P, E])
        picked = sb("picked", [P, E])
        picked_sum = sb("picked_sum", [P, 1])
        inv_gate_sum = sb("inv_gate_sum", [P, 1])
        denom = sb("denom", [P, 1])
        inv_denom = sb("inv_denom", [P, 1])
        gates = sb("gates", [P, TILES_PAIR, E])
        gatesT = sb("gatesT", [E, P])
        hT = sb("hT", [P, HT_BUFS, TILES_PAIR * P])

        sc = [ps(f"sc{i}", [P, GROUPS, S]) for i in range(2)]
        pt = [ps(f"pt{i}", [P, GROUPS * P]) for i in range(2)]
        tile_ps = ps("tile_ps", [P, 512])
        prep_ps = ps("prep_ps", [P, 512])
        h_ps = [sc[0][:, 2 * i:2 * i + 2, :].rearrange("p a b -> p (a b)") for i in range(2)]
        o_ps = [sc[1][:, 2 * i:2 * i + 2, :].rearrange("p a (c d) -> p (a c) d", d=D) for i in range(2)]

        x_loaded = sem("x_loaded")
        const_loaded = sem("const_loaded")
        er_loaded = sem("er_loaded")
        wq_loaded = sem("wq_loaded")
        kv_loaded = sem("kv_loaded")
        ffn_loaded = sem("ffn_loaded")
        stored = sem("stored")
        er_zeroed = sem("er_zeroed")
        filled = sem("filled")
        mask_ready = sem("mask_ready")
        var_ready = sem("var_ready")
        rstd_ready = sem("rstd_ready")
        xn_ready = sem("xn_ready")
        prep_done = sem("prep_done")
        prep_copied = sem("prep_copied")
        rows_copied = sem("rows_copied")
        expanded = sem("expanded")
        heads0_ready = sem("heads0_ready")
        heads1_ready = sem("heads1_ready")
        scores_done = sem("scores_done")
        max_ready = sem("max_ready")
        exp_done = sem("exp_done")
        turned = sem("turned")
        turned_copied = sem("turned_copied")
        pv_done = sem("pv_done")
        pv_used = sem("pv_used")
        var2_ready = sem("var2_ready")
        rstd2_ready = sem("rstd2_ready")
        xn2_ready = sem("xn2_ready")
        tile_done = sem("tile_done")
        tile_copied = sem("tile_copied")
        top_ready = sem("top_ready")
        gate_exp_ready = sem("gate_exp_ready")
        gates_ready = sem("gates_ready")
        h_done = sem("h_done")
        relu_done = sem("relu_done")
        expert_done = sem("expert_done")
        added = sem("added")
        dve_chain = sem("dve_chain")

        block = ctx.enter_context(nc.Block())

        @block.sync
        def _(sp):
            sp.dma_start(x_sb[:, :, :], t["x"].rearrange("b (s p) d -> p (b s) d", p=P)).then_inc(x_loaded, 16)
            sp.dma_start(wqT[:, :], t["wqT"]).then_inc(wq_loaded, 16)
            sp.dma_start(bq_row[:, :], t["bq"]).then_inc(wq_loaded, 16)
            sp.dma_start(ctxT[:, :], t["ctxT"]).then_inc(kv_loaded, 16)
            sp.dma_start(wkT[:, :], t["wkT"]).then_inc(kv_loaded, 16)
            sp.dma_start(wvT[:, :], t["wvT"]).then_inc(kv_loaded, 16)
            sp.dma_start(bk_col[:, :], t["bk"]).then_inc(kv_loaded, 16)
            sp.dma_start(bv_row[:, :], t["bv"]).then_inc(kv_loaded, 16)
            sp.wait_ge(er_zeroed, 1)
            for r in range(ROWS):
                sp.dma_start(er_shift[DH * r:DH * (r + 1), r:r + S], t["erT"]).then_inc(er_loaded, 16)
            sp.dma_start(w1[:, :, :], t["w1"].rearrange("e d h -> d e h")).then_inc(ffn_loaded, 16)
            sp.dma_start(w2[:, :, :], t["w2"].rearrange("e (c p) d -> p (e c) d", p=P)).then_inc(ffn_loaded, 16)
            sp.dma_start(b1_col[:, :], t["b1T"]).then_inc(ffn_loaded, 16)
            sp.dma_start(b2_sb[:, :], t["b2"]).then_inc(ffn_loaded, 16)
            sp.dma_start(gate_sb[:, :], t["gate"]).then_inc(ffn_loaded, 16)
            out = t["out"].rearrange("b (s p) d -> p (b s) d", p=P)
            for pair in range(PAIRS):
                sp.wait_ge(added, E * (pair + 1))
                u0 = TILES_PAIR * pair
                sp.dma_start(out[:, u0:u0 + TILES_PAIR, :], x1[:, u0:u0 + TILES_PAIR, :]).then_inc(stored, 16)
            sp.wait_ge(stored, 16 * PAIRS)

        @block.gpsimd
        def _(pool):
            pool.memset(er_shift[:, :], 0.0).then_inc(er_zeroed, 1)
            pool.memset(minus_half[:, :], -0.5).then_inc(filled, 1)
            pool.memset(ones_row[:, :], 1.0).then_inc(filled, 1)
            pool.memset(v_one[:, :, :, DH:DH + 1], 1.0).then_inc(filled, 1)
            pool.memset(probsT[:, :, :, :], 0.0).then_inc(filled, 1)
            pool.wait_ge(filled, 1)
            pool.wait_ge(var_ready, 1)
            pool.tensor_tensor(rstd[:, :], var_eps[:, :], minus_half[:, :], ALU.pow).then_inc(rstd_ready, 1)

            def expand(u):
                s = u % 2
                if s == 0:
                    pool.wait_ge(prep_copied, 4 * (u // 2) + Q + 1)
                if u >= 2:
                    pool.wait_ge(prep_done, 8 * (u // 2 - 1) + (ROWS_1 if s == 0 else ROWS_3) + 1)
                pool.tensor_tensor(
                    q_expand[:, s, :, :].rearrange("p h (r d) -> p h r d", r=ROWS),
                    q_sb[:, s, :].rearrange("p (h d) -> p h d", h=H).unsqueeze(2).to_broadcast([P, H, ROWS, DH]),
                    row_mask.unsqueeze(1).unsqueeze(3).to_broadcast([P, H, ROWS, DH]),
                    ALU.mult).then_inc(expanded, 1)

            def heads1(b):
                pool.wait_ge(prep_copied, 4 * b + Q_T + 1)
                pool.tensor_tensor(
                    q_heads[:, b % 2, 1, :, :, :],
                    qT[:, 1, :].rearrange("p (g r) -> p g r", r=ROWS).unsqueeze(2).to_broadcast([P, P // ROWS, H, ROWS]),
                    head_mask.unsqueeze(1).unsqueeze(3).to_broadcast([P, P // ROWS, H, ROWS]),
                    ALU.mult).then_inc(heads1_ready, 1)

            def power(u):
                pool.wait_ge(var2_ready, u + 1)
                pool.tensor_tensor(rstd2[:, :], var_eps2[:, :], minus_half[:, 0:1], ALU.pow).then_inc(rstd2_ready, 1)

            pool.wait_ge(const_loaded, 32)
            expand(0)
            expand(1)
            heads1(0)
            for b in range(B):
                if b + 1 < B:
                    expand(2 * b + 2)
                    expand(2 * b + 3)
                power(2 * b)
                if b + 1 < B:
                    heads1(b + 1)
                power(2 * b + 1)

        @block.tensor
        def _(pe):
            def prep(b, step):
                base = 8 * b
                if step == LN_T:
                    pe.wait_ge(xn_ready, TILES)
                    if b > 0:
                        pe.wait_ge(rows_copied, 4 * b)
                    for s in range(2):
                        mm = pe.transpose(prep_ps[:, s * P:(s + 1) * P], xn[:, 2 * b + s, :], ident)
                elif step == KV:
                    pe.wait_ge(prep_copied, 4 * b + KV)
                    pe.wait_ge(kv_loaded, 80)
                    pe.matmul(prep_ps[:, 0:S], wkT[:, :], ctxT[:, b * S:(b + 1) * S], start=True, stop=True)
                    for s in range(2):
                        out = prep_ps[:, S + s * P:S + (s + 1) * P]
                        pe.matmul(out, ctxT[:, b * S + s * P:b * S + (s + 1) * P], wvT[:, :], start=True, stop=False)
                        mm = pe.matmul(out, ones_row[:, :], bv_row[:, :], start=False, stop=True)
                elif step == Q:
                    pe.wait_ge(prep_copied, 4 * b + Q)
                    pe.wait_ge(wq_loaded, 32)
                    for s in range(2):
                        out = prep_ps[:, s * P:(s + 1) * P]
                        pe.matmul(out, xnT[:, s * P:(s + 1) * P], wqT[:, :], start=True, stop=False)
                        mm = pe.matmul(out, ones_row[:, :], bq_row[:, :], start=False, stop=True)
                elif step == Q_T:
                    pe.wait_ge(prep_copied, 4 * b + Q_T)
                    for s in range(2):
                        mm = pe.transpose(prep_ps[:, s * P:(s + 1) * P], q_sb[:, s, :], ident)
                else:
                    i = step - ROWS_0
                    s = i // 2
                    if i == 0:
                        pe.wait_ge(prep_copied, 4 * b + 4)
                    else:
                        pe.wait_ge(rows_copied, 4 * b + i)
                    pe.wait_ge(expanded, 2 * b + s + 1)
                    for j in range(4):
                        h = 8 * (i % 2) + 2 * j
                        pair = q_expand[:, s, h:h + 2, :].rearrange("p h c -> p (h c)")
                        mm = pe.transpose(prep_ps[:, j * P:(j + 1) * P], pair, ident)
                mm.then_inc(prep_done, 1)

            def scores(n):
                b, k = divmod(n, PER_BATCH)
                s = k // PER_TILE
                if k % PER_TILE == 0:
                    pe.wait_ge(rows_copied, 4 * b + 2 * s + 2)
                    if s == 0:
                        pe.wait_ge(heads0_ready, b + 1)
                    else:
                        pe.wait_ge(heads1_ready, b + 1)
                if n == 0:
                    pe.wait_ge(er_loaded, 16 * ROWS)
                    pe.wait_ge(mask_ready, 1)
                if n >= 2:
                    pe.wait_ge(exp_done, n - 1)
                if n % BLOCKS_PAIR == 0 and n:
                    pair = n // BLOCKS_PAIR
                    pe.wait_ge(relu_done, CHUNKS * pair)
                    pe.wait_ge(added, E * pair)
                keys = BLOCK * (k + 1)
                for g in range(GROUPS):
                    row0 = BLOCK * k + ROWS * g
                    seen = row0 + ROWS
                    group = (row0 - P * s) // ROWS
                    pe.matmul(sc[n % 2][:, g, 0:seen], q_rows[:, b % 2, s, group, :, :].rearrange("p h r -> p (h r)"),
                              er_shift[:, S - 1 - row0:S - 1 - row0 + seen],
                              start=True, stop=False, skip_group_check=True)
                    pe.matmul(sc[n % 2][:, g, 0:seen], q_heads[:, b % 2, s, group, :, :].rearrange("p h r -> p (h r)"),
                              kT[:, b, 0:seen], start=False, stop=False, skip_group_check=True)
                    mm = pe.matmul(sc[n % 2][:, g, row0:keys], mask_rows, mask_keys[:, 0:keys - row0],
                                   start=False, stop=True, skip_group_check=True)
                mm.then_inc(scores_done, 1)

            def turn(n):
                pe.wait_ge(exp_done, n + 1)
                for c, key0, keys in units_of(n):
                    unit = UNITS_BEFORE[n] + c
                    if unit >= 2:
                        pe.wait_ge(turned_copied, unit - 1)
                    for g in range(GROUPS):
                        mm = pe.transpose(pt[unit % 2][0:keys, g * P:(g + 1) * P],
                                          probs[:, n % 3, g, key0:key0 + keys], ident)
                    mm.then_inc(turned, 1)

            def values(u):
                b, s = divmod(u, 2)
                pe.wait_ge(turned_copied, UNITS_BEFORE[PER_TILE * (u + 1)])
                if u:
                    pe.wait_ge(tile_copied, 4 * u)
                pe.wait_ge(prep_copied, 4 * b + KV + 1)
                for h in range(H):
                    for c in range(s + 1):
                        mm = pe.matmul(tile_ps[:, (DH + 1) * h:(DH + 1) * (h + 1)],
                                       probsT[:, s + c, h, :], v_one[:, 2 * b + c, h, :],
                                       start=(c == 0), stop=(c == s))
                mm.then_inc(pv_done, 1)

            def tile(u, step):
                if step == LN2_T:
                    pe.wait_ge(pv_used, u + 1)
                    pe.wait_ge(xn2_ready, u + 1)
                    mm = pe.transpose(tile_ps[:, 0:P], xn2[:, :], ident)
                elif step == GATE:
                    pe.wait_ge(tile_copied, 4 * u + GATE)
                    pe.wait_ge(ffn_loaded, 80)
                    mm = pe.matmul(tile_ps[:, 0:E], xn2T[:, u % TILES_PAIR, :], gate_sb[:, :], start=True, stop=True)
                elif step == GATE_T:
                    pe.wait_ge(tile_copied, 4 * u + GATE_T)
                    pe.wait_ge(gates_ready, u + 1)
                    mm = pe.transpose(tile_ps[0:E, 0:P], gates[:, u % TILES_PAIR, :], ident)
                else:
                    pe.wait_ge(tile_copied, 4 * u + BIAS2)
                    mm = pe.matmul(tile_ps[:, 0:D], gatesT[:, :], b2_sb[:, :], start=True, stop=True)
                mm.then_inc(tile_done, 1)

            def hidden(pair, c):
                i = CHUNKS * pair + c
                if i >= 2:
                    pe.wait_ge(relu_done, i - 1)
                mm = pe.matmul(h_ps[c % 2], w1[:, c // 2, P * (c % 2):P * (c % 2 + 1)],
                               xn2T[:, :, :].rearrange("p t n -> p (t n)"), start=True, stop=True)
                mm.then_inc(h_done, 1)

            def experts(pair, e):
                i = E * pair + e
                pe.wait_ge(relu_done, CHUNKS * pair + 2 * e + 2)
                if i >= 2:
                    pe.wait_ge(added, i - 1)
                for tt in range(TILES_PAIR):
                    for c in range(2):
                        mm = pe.matmul(o_ps[e % 2][:, tt, :],
                                       hT[:, (2 * e + c) % HT_BUFS, tt * P:(tt + 1) * P],
                                       w2[:, 2 * e + c, :], start=(c == 0), stop=(c == 1))
                mm.then_inc(expert_done, 1)

            pe.wait_ge(const_loaded, 32)
            pe.wait_ge(filled, 4)
            for step in range(8):
                prep(0, step)
            for pair in range(PAIRS):
                first = BLOCKS_PAIR * pair
                for n in range(first, first + BLOCKS_PAIR):
                    scores(n)
                    if n // PER_BATCH + 1 < B:
                        prep(n // PER_BATCH + 1, n % PER_BATCH)
                    u, step = divmod(n - 5, PER_TILE)
                    if u >= TILES_PAIR * pair:
                        tile(u, step)
                    if n > first:
                        turn(n - 1)
                        if n % PER_TILE == 0:
                            values(n // PER_TILE - 1)
                last = TILES_PAIR * (pair + 1) - 1
                turn(first + BLOCKS_PAIR - 1)
                tile(last - 1, BIAS2)
                values(last)
                tile(last, LN2_T)
                tile(last, GATE)
                hidden(pair, 0)
                hidden(pair, 1)
                tile(last, GATE_T)
                hidden(pair, 2)
                tile(last, BIAS2)
                hidden(pair, 3)
                for e in range(E):
                    experts(pair, e)
                    if e + 2 < E:
                        hidden(pair, 2 * e + 4)
                        hidden(pair, 2 * e + 5)

        @block.scalar
        def _(act):
            act.dma_start(wide[:, :], t["const_wide"]).then_inc(const_loaded, 16)
            act.dma_start(mask_f32[:, :], t["const_mask"]).then_inc(const_loaded, 16)

            def rows_out(b, i):
                act.wait_ge(prep_done, 8 * b + ROWS_0 + i + 1)
                s, h0 = i // 2, 8 * (i % 2)
                src = prep_ps[:, :].rearrange("p (j g r) -> p j g r", j=4, r=ROWS)
                dst = q_rows[:, b % 2, s, :, h0:h0 + 8, :].rearrange("p g (j o) r -> p o j g r", o=2)
                act.activation(dst[:, 0, :, :, :], src[0:64, :, :, :], ACT.Copy)
                act.activation(dst[:, 1, :, :, :], src[64:128, :, :, :], ACT.Copy).then_inc(rows_copied, 1)

            def exponents(n):
                act.wait_ge(max_ready, n + 1)
                if n >= 3:
                    act.wait_ge(turned, UNITS_BEFORE[n - 2])
                keys = BLOCK * (n % PER_BATCH + 1)
                for g in range(GROUPS):
                    last = act.activation(probs[:, n % 3, g, 0:keys], sc[n % 2][:, g, 0:keys], ACT.Exp,
                                          bias=neg_max[:, n % 4, g:g + 1])
                last.then_inc(exp_done, 1)

            def gate_exponents(u):
                act.wait_ge(top_ready, u + 1)
                act.activation(gate_exp[:, :], logits[:, :], ACT.Exp, bias=neg_top[:, :],
                               accum_out=gate_sum[:, :]).then_inc(gate_exp_ready, 1)

            def relu(pair, c):
                i = CHUNKS * pair + c
                act.wait_ge(h_done, i + 1)
                if i >= HT_BUFS:
                    act.wait_ge(expert_done, (i - HT_BUFS) // 2 + 1)
                if i == 0:
                    act.wait_ge(ffn_loaded, 80)
                act.activation(hT[:, c % HT_BUFS, :], h_ps[c % 2], ACT.Relu,
                               bias=b1_col[:, c:c + 1]).then_inc(relu_done, 1)

            for i in range(4):
                rows_out(0, i)
            for pair in range(PAIRS):
                first = BLOCKS_PAIR * pair
                for n in range(first, first + BLOCKS_PAIR):
                    exponents(n)
                    b, k = divmod(n, PER_BATCH)
                    if b + 1 < B and k >= ROWS_0:
                        rows_out(b + 1, k - ROWS_0)
                    u, step = divmod(n - 5, PER_TILE)
                    if step == GATE and u >= TILES_PAIR * pair:
                        gate_exponents(u)
                gate_exponents(TILES_PAIR * (pair + 1) - 1)
                for c in range(CHUNKS):
                    relu(pair, c)

        @block.vector
        def _(dve):
            chain = [0]

            def link(ins):
                chain[0] += 1
                ins.then_inc(dve_chain, 1)
                dve.wait_ge(dve_chain, chain[0])

            def prep_out(b, step):
                dve.wait_ge(prep_done, 8 * b + step + 1)
                if step == LN_T:
                    dve.tensor_copy(xnT[:, :], prep_ps[:, 0:S]).then_inc(prep_copied, 1)
                elif step == KV:
                    dve.tensor_scalar(kT[:, b, :], prep_ps[:, 0:S], bk_col[:, 0:1], None, ALU.add)
                    dve.tensor_copy(v_one[:, 2 * b:2 * b + 2, :, 0:DH],
                                    prep_ps[:, S:2 * S].rearrange("p (s h d) -> p s h d", s=2, h=H)
                                    ).then_inc(prep_copied, 1)
                elif step == Q:
                    dve.tensor_scalar(q_sb[:, :, :].rearrange("p s d -> p (s d)"), prep_ps[:, 0:S], SCALE, None,
                                      ALU.mult).then_inc(prep_copied, 1)
                elif step == Q_T:
                    if b:
                        dve.wait_ge(heads1_ready, b)
                    dve.tensor_copy(qT[:, :, :].rearrange("p s n -> p (s n)"), prep_ps[:, 0:S]
                                    ).then_inc(prep_copied, 1)

            def heads0(b):
                dve.wait_ge(prep_copied, 4 * b + 4)
                dve.tensor_tensor(
                    q_heads[:, b % 2, 0, :, :, :],
                    qT[:, 0, :].rearrange("p (g r) -> p g r", r=ROWS).unsqueeze(2).to_broadcast([P, P // ROWS, H, ROWS]),
                    head_mask.unsqueeze(1).unsqueeze(3).to_broadcast([P, P // ROWS, H, ROWS]),
                    ALU.mult).then_inc(heads0_ready, 1)

            def maxima(n):
                dve.wait_ge(scores_done, n + 1)
                keys = BLOCK * (n % PER_BATCH + 1)
                dve.tensor_reduce(neg_max[:, n % 4, :], sc[n % 2][:, :, 0:keys], AX.X, ALU.max,
                                  negate=True).then_inc(max_ready, 1)

            def turned_out(n):
                k = n % PER_BATCH
                q0 = BLOCK * (k % PER_TILE)
                for c, key0, keys in units_of(n):
                    unit = UNITS_BEFORE[n] + c
                    dve.wait_ge(turned, unit + 1)
                    dst = probsT[0:keys, k // PER_TILE + c, :, q0:q0 + BLOCK]
                    dve.tensor_copy(dst.rearrange("p h (g r) -> p g h r", g=GROUPS),
                                    pt[unit % 2][0:keys, :].rearrange("p (g h r) -> p g h r", g=GROUPS, h=H)
                                    ).then_inc(turned_copied, 1)

            def residual(u):
                dve.wait_ge(pv_done, u + 1)
                pv = tile_ps[:, 0:H * (DH + 1)].rearrange("p (h c) -> p h c", h=H)
                link(dve.reciprocal(inv_sum[:, :], pv[:, :, DH]))
                dve.tensor_tensor(attn[:, :, :], pv[:, :, 0:DH],
                                  inv_sum[:, :].unsqueeze(2).to_broadcast([P, H, DH]), ALU.mult).then_inc(pv_used, 1)
                dve.wait_ge(pv_used, u + 1)
                link(dve.tensor_tensor(x1[:, u, :], attn[:, :, :].rearrange("p h d -> p (h d)"), x_sb[:, u, :],
                                       ALU.add))
                link(dve.bn_stats(stats2[:, :], x1[:, u, :]))
                link(dve.bn_aggr(mean_var2[:, :], stats2[:, :]))
                dve.tensor_scalar(var_eps2[:, :], mean_var2[:, 1:2], EPS, None, ALU.add).then_inc(var2_ready, 1)

            def norm2(u):
                dve.wait_ge(rstd2_ready, u + 1)
                if u:
                    dve.wait_ge(tile_done, 4 * (u - 1) + LN2_T + 1)
                dve.tensor_scalar(xn2[:, :], x1[:, u, :], mean_var2[:, 0:1], rstd2[:, 0:1], ALU.subtract,
                                  ALU.mult).then_inc(xn2_ready, 1)

            def tile_out(u, step):
                dve.wait_ge(tile_done, 4 * u + step + 1)
                if step == LN2_T:
                    dve.tensor_copy(xn2T[:, u % TILES_PAIR, :], tile_ps[:, 0:P]).then_inc(tile_copied, 1)
                elif step == GATE:
                    dve.tensor_copy(logits[:, :], tile_ps[:, 0:E]).then_inc(tile_copied, 1)
                    dve.wait_ge(tile_copied, 4 * u + GATE + 1)
                    link(dve.max(sorted8[:, :], logits[:, :]))
                    dve.tensor_scalar(neg_top[:, :], sorted8[:, 0:1], -1.0, None, ALU.mult).then_inc(top_ready, 1)
                elif step == GATE_T:
                    dve.tensor_copy(gatesT[:, :], tile_ps[0:E, 0:P]).then_inc(tile_copied, 1)
                else:
                    dve.tensor_tensor(x1[:, u, :], tile_ps[:, 0:D], x1[:, u, :], ALU.add).then_inc(tile_copied, 1)

            def pick(u):
                link(dve.tensor_tensor(diff[:, :, :], logits[:, :].unsqueeze(1).to_broadcast([P, E, E]),
                                       logits[:, :].unsqueeze(2).to_broadcast([P, E, E]), ALU.subtract))
                link(dve.scalar_tensor_tensor(out=above[:, :, :], in0=diff[:, :, :], scalar=-1.0, in1=tie_tri,
                                              op0=ALU.mult, op1=ALU.is_lt))
                link(dve.tensor_reduce(rank[:, :], above[:, :, :], AX.X, ALU.add))
                dve.wait_ge(gate_exp_ready, u + 1)
                link(dve.scalar_tensor_tensor(out=picked[:, :], in0=rank[:, :], scalar=2.0, in1=gate_exp[:, :],
                                              op0=ALU.is_lt, op1=ALU.mult, accum_out=picked_sum[:, :]))
                link(dve.reciprocal(inv_gate_sum[:, :], gate_sum[:, :]))
                link(dve.tensor_scalar(denom[:, :], picked_sum[:, :], inv_gate_sum[:, 0:1], 1e-12, ALU.mult, ALU.max))
                link(dve.reciprocal(inv_denom[:, :], denom[:, :]))
                dve.tensor_scalar(gates[:, u % TILES_PAIR, :], picked[:, :], inv_gate_sum[:, 0:1],
                                  inv_denom[:, 0:1], ALU.mult, ALU.mult).then_inc(gates_ready, 1)

            def add_expert(pair, e):
                i = E * pair + e
                dve.wait_ge(expert_done, i + 1)
                if e:
                    dve.wait_ge(added, i)
                else:
                    dve.wait_ge(tile_copied, 4 * TILES_PAIR * (pair + 1))
                for tt in range(TILES_PAIR):
                    u = TILES_PAIR * pair + tt
                    last = dve.scalar_tensor_tensor(out=x1[:, u, :], in0=o_ps[e % 2][:, tt, :],
                                                    scalar=gates[:, tt, e:e + 1], in1=x1[:, u, :],
                                                    op0=ALU.mult, op1=ALU.add)
                last.then_inc(added, 1)

            dve.wait_ge(x_loaded, 16)
            for u in range(TILES):
                ins = dve.bn_stats(stats[:, u, :], x_sb[:, u, :])
            link(ins)
            for u in range(TILES):
                ins = dve.bn_aggr(mean_var[:, u, :], stats[:, u, :])
            link(ins)
            dve.tensor_scalar(var_eps[:, :], mean_var[:, :, 1], EPS, None, ALU.add).then_inc(var_ready, 1)
            dve.wait_ge(const_loaded, 32)
            dve.tensor_copy(mask_b16[:, :], mask_f32[:, :]).then_inc(mask_ready, 1)
            dve.wait_ge(rstd_ready, 1)
            for u in range(TILES):
                dve.tensor_scalar(xn[:, u, :], x_sb[:, u, :], mean_var[:, u, 0:1], rstd[:, u:u + 1], ALU.subtract,
                                  ALU.mult).then_inc(xn_ready, 1)
            dve.wait_ge(kv_loaded, 80)
            dve.wait_ge(filled, 4)
            for step in range(4):
                prep_out(0, step)
            heads0(0)
            for pair in range(PAIRS):
                first = BLOCKS_PAIR * pair
                for n in range(first, first + BLOCKS_PAIR):
                    b, k = divmod(n, PER_BATCH)
                    u, step = divmod(n - 5, PER_TILE)
                    if u < TILES_PAIR * pair:
                        step = None
                    if step == LN2_T:
                        norm2(u)
                    if step == GATE_T:
                        pick(u)
                    maxima(n)
                    if b + 1 < B and k < 4:
                        prep_out(b + 1, k)
                    if b + 1 < B and k == 5:
                        heads0(b + 1)
                    if step is not None:
                        tile_out(u, step)
                    if n > first:
                        turned_out(n - 1)
                        if n % PER_TILE == 0:
                            residual(n // PER_TILE - 1)
                last = TILES_PAIR * (pair + 1) - 1
                turned_out(first + BLOCKS_PAIR - 1)
                tile_out(last - 1, BIAS2)
                residual(last)
                norm2(last)
                tile_out(last, LN2_T)
                tile_out(last, GATE)
                pick(last)
                tile_out(last, GATE_T)
                tile_out(last, BIAS2)
                for e in range(E):
                    add_expert(pair, e)


def kernel(x, ctx_1024, L0_xattn_Wq, L0_xattn_bq, L0_xattn_Wk, L0_xattn_bk, L0_xattn_Wv, L0_xattn_bv,
           L0_xattn_Er, L0_ffn_gate, L0_ffn_W1, L0_ffn_b1, L0_ffn_W2, L0_ffn_b2):
    import concourse.bacc as bacc
    from concourse.bass_utils import run_bass_kernel_spmd

    a = lambda v: np.ascontiguousarray(np.asarray(v))
    arrays = {
        "x": a(x),
        "ctxT": a(np.asarray(ctx_1024).reshape(B * S, D).T),
        "wqT": a(np.asarray(L0_xattn_Wq).T),
        "wkT": a(np.asarray(L0_xattn_Wk).T),
        "wvT": a(np.asarray(L0_xattn_Wv).T),
        "bq": a(L0_xattn_bq).reshape(1, D),
        "bk": a(L0_xattn_bk).reshape(D, 1),
        "bv": a(L0_xattn_bv).reshape(1, D),
        "erT": a(np.asarray(L0_xattn_Er).T),
        "gate": a(L0_ffn_gate),
        "w1": a(L0_ffn_W1),
        "b1T": a(np.asarray(L0_ffn_b1).reshape(CHUNKS, P).T),
        "w2": a(L0_ffn_W2),
        "b2": a(L0_ffn_b2),
    }
    arrays.update(shape_constants())
    nc = bacc.Bacc("TRN2", target_bir_lowering=False, num_devices=1)
    t = {k: nc.dram_tensor("in_" + k, v.shape, mybir.dt.from_np(v.dtype), kind="ExternalInput").ap()
         for k, v in arrays.items()}
    t["out"] = nc.dram_tensor("out", (B, S, D), F32, kind="ExternalOutput").ap()
    build(nc, t)
    r = run_bass_kernel_spmd(nc, [{"in_" + k: v for k, v in arrays.items()}], core_ids=[0])
    return r.results[0]["out"]
```

```python
from contextlib import ExitStack

import numpy as np

from concourse import mybir

F32 = mybir.dt.float32
BF16 = mybir.dt.bfloat16
ALU = mybir.AluOpType
ACT = mybir.ActivationFunctionType
AX = mybir.AxisListType

B, S, D, H, DH = 4, 256, 128, 16, 8
E, HID = 8, 256
P = 128
TILES = B * S // P
ROWS = 8
GROUPS = 4
BLOCK = ROWS * GROUPS
BLOCKS = B * S // BLOCK
PER_BATCH = S // BLOCK
PER_TILE = P // BLOCK
CHUNKS = 2 * E
K_ROWS = ROWS * DH + ROWS
ER_W = S + BLOCK
MASKED = -1e30
EPS = 1e-5
SCALE = float(DH) ** -0.5
TIE = 1.2e-38
HT_BUFS = 3


def shape_constants():
    part = np.arange(P)
    row_mask = (part[:, None] % ROWS == np.arange(ROWS)).astype(np.float32)
    head_mask = (part[:, None] // DH == np.arange(H)).astype(np.float32)
    mask_rows = (np.arange(ROWS)[:, None] == np.tile(np.arange(ROWS), H)).astype(np.float32)
    mask_er = np.where(np.arange(ER_W)[None, :] - np.arange(ROWS)[:, None] >= S, MASKED, 0.0).astype(np.float32)
    i, j = np.meshgrid(np.arange(E), np.arange(E), indexing="ij")
    tie = np.broadcast_to(np.where(j < i, TIE, 0.0).astype(np.float32).reshape(1, E * E), (P, E * E))
    wide = np.concatenate([np.eye(P, dtype=np.float32), row_mask, head_mask, tie], axis=1)
    return {"const_wide": np.ascontiguousarray(wide), "const_rows": mask_rows, "const_er": mask_er}


MIXED = [0, 7, 1, 6, 2, 5, 3, 4]
ORDER = [(b, k) for b in range(B) for k in MIXED]
TILE_OF = [2 * b + k // PER_TILE for b, k in ORDER]
FIRST_BLOCK = [TILE_OF.index(u) for u in range(TILES)]
LAST_BLOCK = [max(n for n in range(BLOCKS) if TILE_OF[n] == u) for u in range(TILES)]

JOBS = [[2 * b, 2 * b + 1] for b in range(B)]


def units_of(n):
    keys = BLOCK * (ORDER[n][1] + 1)
    return [(c, c * P, min(P, keys - c * P)) for c in range((keys + P - 1) // P)]


LAG = 1
FFN_AFTER = [8 * b + 11 + 2 * LAG for b in range(B - 2)]

UNITS_BEFORE = [0]
for _n in range(BLOCKS):
    UNITS_BEFORE.append(UNITS_BEFORE[-1] + len(units_of(_n)))

KV, LN_T, Q, Q_T, ROWS_0, ROWS_1, ROWS_2, ROWS_3 = range(8)
VALUES_T, LN2_T, GATE, GATE_T = range(4)
VW = 32
WARM = (12, 1, 3, 3, 7, 0, 2)

PREP_AT = [[(n // PER_BATCH + 1, n % PER_BATCH)] if n // PER_BATCH + 1 < B else [] for n in range(BLOCKS)]

VALUES_AT = {PER_BATCH * (_u // 2) + PER_BATCH - 1 + _u % 2 + LAG: _u for _u in range(TILES - 2)}
TILE_AT = [[] for n in range(BLOCKS)]
for _j in range(B - 1):
    for _i, _job_step in enumerate([(_j, VALUES_T, 2 * _j), (_j, VALUES_T, 2 * _j + 1), (_j, LN2_T, None),
                                    (_j, GATE, None), (_j, GATE_T, None)]):
        TILE_AT[PER_BATCH * (_j + 1) + LAG + _i].append(_job_step)


def tile_count(j, step, u=None):
    before = sum(len(tiles) + 3 for tiles in JOBS[:j])
    return before + (JOBS[j].index(u) + 1 if step == VALUES_T else len(JOBS[j]) + step)


def build(nc, t):
    ctx = ExitStack()
    with ctx:
        def sb(name, shape, dt=F32):
            return ctx.enter_context(nc.sbuf_tensor(name, shape, dt))

        def ps(name, shape, dt=F32):
            return ctx.enter_context(nc.psum_tensor(name, shape, dt))

        def sem(name):
            return ctx.enter_context(nc.semaphore(name))

        x_sb = sb("x_sb", [P, TILES, D])
        ctxT = sb("ctxT", [D, B * S])
        wqT = sb("wqT", [D, D])
        wkT = sb("wkT", [D, D])
        wvT = sb("wvT", [D, D])
        bq_all = sb("bq_all", [P, D])
        bq_scaled = sb("bq_scaled", [P, D])
        bv_all = sb("bv_all", [P, D])
        bk_col = sb("bk_col", [D, 1])
        er_shift = sb("er_shift", [K_ROWS, ER_W])
        wide = sb("wide", [P, P + ROWS + H + E * E])
        ident = wide[:, 0:P]
        row_mask = wide[:, P:P + ROWS]
        head_mask = wide[:, P + ROWS:P + ROWS + H]
        tie_tri = wide[:, P + ROWS + H:].rearrange("p (i j) -> p i j", i=E)
        w1 = sb("w1", [D, E, HID])
        w2 = sb("w2", [P, CHUNKS, D])
        b1_col = sb("b1_col", [P, CHUNKS])
        b2_sb = sb("b2_sb", [E, D])
        gate_sb = sb("gate_sb", [D, E])

        stats = sb("stats", [P, TILES, 6])
        mean_var = sb("mean_var", [P, TILES, 2])
        var_eps = sb("var_eps", [P, TILES])
        rstd = sb("rstd", [P, TILES])
        minus_half = sb("minus_half", [P, TILES])
        xn = sb("xn", [P, TILES, D])
        xnT = sb("xnT", [D, S])
        kT = sb("kT", [D, B, S])
        v_one = sb("v_one", [P, TILES, H, VW])
        q_sb = sb("q_sb", [P, 2, D])
        qT = sb("qT", [D, 2, P])
        q_expand = sb("q_expand", [P, 2, H, ROWS * DH])
        q_rows = sb("q_rows", [K_ROWS, 2, 2, P // ROWS, H, ROWS])
        q_heads = sb("q_heads", [D, 2, 2, P // ROWS, H, ROWS])
        neg_max = sb("neg_max", [P, 4, GROUPS])
        probs = sb("probs", [P, 3, GROUPS, S])
        probsT = sb("probsT", [P, 3, H, P])
        inv_sum = sb("inv_sum", [P, H])
        pv_sb = sb("pv_sb", [P, 2, H // 4, P])
        attn = sb("attn", [P, H, DH])
        x1 = sb("x1", [P, TILES, D])
        stats2 = sb("stats2", [P, 2, 6])
        mean_var2 = sb("mean_var2", [P, 2, 2])
        var_eps2 = sb("var_eps2", [P, 2])
        rstd2 = sb("rstd2", [P, 2])
        xn2 = sb("xn2", [P, 2, D])
        xn2T = sb("xn2T", [D, TILES, P])
        logits = sb("logits", [P, 2, E])
        sorted8 = sb("sorted8", [P, 2, E])
        neg_top = sb("neg_top", [P, 2])
        gate_exp = sb("gate_exp", [P, 2, E])
        gate_sum = sb("gate_sum", [P, 2])
        diff = sb("diff", [P, 2, E, E])
        above = sb("above", [P, 2, E, E])
        rank = sb("rank", [P, 2, E])
        picked = sb("picked", [P, 2, E])
        picked_sum = sb("picked_sum", [P, 2])
        inv_gate_sum = sb("inv_gate_sum", [P, 2])
        denom = sb("denom", [P, 2])
        guarded = sb("guarded", [P, 2])
        inv_denom = sb("inv_denom", [P, 2])
        gates = sb("gates", [P, TILES, E])
        gatesT = sb("gatesT", [E, TILES, P])
        zeros = sb("zeros", [P, P + 512], BF16)
        hT = sb("hT", [P, HT_BUFS, 2, S])

        sc = [ps(f"sc{i}", [P, GROUPS, S]) for i in range(2)]
        pt = [ps(f"pt{i}", [P, GROUPS * P]) for i in range(2)]
        tile_ps = ps("tile_ps", [P, 512])
        prep_ps = ps("prep_ps", [P, 512])
        h_ps = [sc[0][:, 2 * i:2 * i + 2, :] for i in range(2)]
        o_ps = [sc[1][:, 2 * i, :].rearrange("p (s d) -> p s d", d=D) for i in range(2)]

        def prep_bank(b, step):
            if b:
                return prep_ps
            return {KV: tile_ps, LN_T: prep_ps, Q: pt[0], Q_T: pt[1],
                    ROWS_0: sc[1][:, 0:2, :].rearrange("p g n -> p (g n)"),
                    ROWS_1: sc[1][:, 2:4, :].rearrange("p g n -> p (g n)"),
                    ROWS_2: tile_ps, ROWS_3: pt[1]}[step]

        x_loaded = sem("x_loaded")
        rest_loaded = sem("rest_loaded")
        const_loaded = sem("const_loaded")
        er_loaded = sem("er_loaded")
        mask_loaded = sem("mask_loaded")
        wq_loaded = sem("wq_loaded")
        kv_loaded = sem("kv_loaded")
        bias_loaded = sem("bias_loaded")
        ffn_loaded = sem("ffn_loaded")
        stored = sem("stored")
        zeroed = sem("zeroed")
        filled = sem("filled")
        bq_ready = sem("bq_ready")
        var_ready = sem("var_ready")
        rstd_ready = sem("rstd_ready")
        xn_ready = sem("xn_ready")
        prep_done = sem("prep_done")
        prep_copied = sem("prep_copied")
        rows_copied = sem("rows_copied")
        expanded0 = sem("expanded0")
        expanded = sem("expanded")
        odd_copied = sem("odd_copied")
        heads0_ready = sem("heads0_ready")
        heads_ready = sem("heads_ready")
        scores_done = sem("scores_done")
        max_ready = sem("max_ready")
        exp_done = sem("exp_done")
        turned = sem("turned")
        turned_copied = sem("turned_copied")
        pv_done = sem("pv_done")
        pv_copied = sem("pv_copied")
        pv_used = sem("pv_used")
        var2_ready = sem("var2_ready")
        rstd2_ready = sem("rstd2_ready")
        xn2_ready = sem("xn2_ready")
        bias2_done = sem("bias2_done")
        bias2_added = sem("bias2_added")
        tile_done = sem("tile_done")
        tile_copied = sem("tile_copied")
        top_ready = sem("top_ready")
        gate_exp_ready = sem("gate_exp_ready")
        gates_ready = sem("gates_ready")
        h_done = sem("h_done")
        relu_done = sem("relu_done")
        expert_done = sem("expert_done")
        added = sem("added")
        dve_chain = sem("dve_chain")

        block = ctx.enter_context(nc.Block())

        @block.sync
        def _(sp):
            x_in = t["x"].rearrange("b (s p) d -> p (b s) d", p=P)
            out = t["out"].rearrange("b (s p) d -> p (b s) d", p=P)
            sp.dma_start(x_sb[:, 0:2, :], x_in[:, 0:2, :]).then_inc(x_loaded, 16)
            sp.dma_start(ctxT[:, 0:S], t["ctxT"][:, 0:S]).then_inc(kv_loaded, 16)
            sp.dma_start(wqT[:, :], t["wqT"]).then_inc(wq_loaded, 16)
            sp.dma_start(er_shift[0:ROWS * DH, :], t["er_rows"]).then_inc(er_loaded, 16)
            sp.dma_start(er_shift[ROWS * DH:K_ROWS, :], t["const_er"]).then_inc(er_loaded, 16)
            sp.dma_start(x_sb[:, 2:TILES, :], x_in[:, 2:TILES, :]).then_inc(rest_loaded, 16)
            sp.dma_start(ctxT[:, S:B * S], t["ctxT"][:, S:B * S]).then_inc(rest_loaded, 16)
            sp.dma_start(w1[:, :, :], t["w1"].rearrange("e d h -> d e h")).then_inc(ffn_loaded, 16)
            sp.dma_start(w2[:, :, :], t["w2"].rearrange("e (c p) d -> p (e c) d", p=P)).then_inc(ffn_loaded, 16)
            sp.dma_start(b1_col[:, :], t["b1T"]).then_inc(ffn_loaded, 16)
            sp.dma_start(b2_sb[:, :], t["b2"]).then_inc(ffn_loaded, 16)
            sp.dma_start(gate_sb[:, :], t["gate"]).then_inc(ffn_loaded, 16)
            for b in range(B):
                sp.wait_ge(added, E * (b + 1))
                sp.dma_start(out[:, 2 * b:2 * b + 2, :], x1[:, 2 * b:2 * b + 2, :]).then_inc(stored, 16)
            sp.wait_ge(stored, 16 * B)

        @block.gpsimd
        def _(pool):
            pool.memset(zeros[:, :], 0.0).then_inc(zeroed, 1)
            pool.memset(minus_half[:, :], -0.5).then_inc(filled, 1)
            pool.memset(v_one[:, :, :, DH:DH + 1], 1.0).then_inc(filled, 1)
            pool.memset(v_one[:, :, :, DH + 1:VW], 0.0).then_inc(filled, 1)
            pool.wait_ge(filled, 3)
            pool.wait_ge(var_ready, 1)
            pool.tensor_tensor(rstd[:, 0:2], var_eps[:, 0:2], minus_half[:, 0:2], ALU.pow).then_inc(rstd_ready, 1)
            pool.memset(probsT[:, 0, :, :], 0.0).then_inc(filled, 1)
            pool.memset(probsT[:, 2, :, :], 0.0).then_inc(filled, 1)

            def expand(u):
                s = u % 2
                if s == 0 or u == 1:
                    pool.wait_ge(prep_copied, 4 * (u // 2) + Q + 1)
                if u >= 2:
                    pool.wait_ge(prep_done, 8 * (u // 2 - 1) + (ROWS_1 if s == 0 else ROWS_3) + 1)
                pool.tensor_tensor(
                    q_expand[:, s, :, :].rearrange("p h (r d) -> p h r d", r=ROWS),
                    q_sb[:, s, :].rearrange("p (h d) -> p h d", h=H).unsqueeze(2).to_broadcast([P, H, ROWS, DH]),
                    row_mask.unsqueeze(1).unsqueeze(3).to_broadcast([P, H, ROWS, DH]),
                    ALU.mult).then_inc(expanded, 1)

            def heads(b, s):
                pool.wait_ge(prep_copied, 4 * b + Q_T + 1)
                pool.tensor_tensor(
                    q_heads[:, b % 2, s, :, :, :],
                    qT[:, s, :].rearrange("p (g r) -> p g r", r=ROWS).unsqueeze(2).to_broadcast([P, P // ROWS, H, ROWS]),
                    head_mask.unsqueeze(1).unsqueeze(3).to_broadcast([P, P // ROWS, H, ROWS]),
                    ALU.mult).then_inc(heads_ready, 1)

            def power(j):
                pool.wait_ge(var2_ready, j + 1)
                w = len(JOBS[j])
                pool.tensor_tensor(rstd2[:, 0:w], var_eps2[:, 0:w], minus_half[:, 0:w], ALU.pow
                                   ).then_inc(rstd2_ready, 1)

            pool.wait_ge(const_loaded, 16)
            expand(1)
            heads(0, 1)
            pool.wait_ge(var_ready, 2)
            pool.tensor_tensor(rstd[:, 2:TILES], var_eps[:, 2:TILES], minus_half[:, 2:TILES], ALU.pow
                               ).then_inc(rstd_ready, 1)
            for b in range(1, B):
                expand(2 * b)
                if b >= 2:
                    power(b - 2)
                heads(b, 0)
                expand(2 * b + 1)
                heads(b, 1)
            power(B - 2)
            power(B - 1)

        @block.tensor
        def _(pe):
            def prep(b, step):
                out_ps = prep_bank(b, step)
                if step == KV:
                    pe.wait_ge(kv_loaded, 48)
                    if b > 1:
                        pe.wait_ge(rows_copied, 4 * b)
                    if b > 0:
                        pe.wait_ge(rest_loaded, 32)
                    pe.matmul(out_ps[:, 0:S], wkT[:, :], ctxT[:, b * S:(b + 1) * S], start=True, stop=True)
                    for s in range(2):
                        out = out_ps[:, S + s * P:S + (s + 1) * P]
                        mm = pe.matmul(out, ctxT[:, b * S + s * P:b * S + (s + 1) * P], wvT[:, :],
                                       start=True, stop=True)
                elif step == LN_T:
                    if b > 0:
                        pe.wait_ge(prep_copied, 4 * b + LN_T)
                    else:
                        pe.wait_ge(const_loaded, 16)
                    pe.wait_ge(xn_ready, 2 * b + 2)
                    for s in range(2):
                        mm = pe.transpose(out_ps[:, s * P:(s + 1) * P], xn[:, 2 * b + s, :], ident)
                elif step == Q:
                    pe.wait_ge(prep_copied, 4 * b + Q)
                    pe.wait_ge(wq_loaded, 16)
                    for s in range(2):
                        out = out_ps[:, s * P:(s + 1) * P]
                        mm = pe.matmul(out, xnT[:, s * P:(s + 1) * P], wqT[:, :], start=True, stop=True)
                elif step == Q_T:
                    pe.wait_ge(prep_copied, 4 * b + Q_T)
                    for s in range(2):
                        mm = pe.transpose(out_ps[:, s * P:(s + 1) * P], q_sb[:, s, :], ident)
                else:
                    i = step - ROWS_0
                    s = i // 2
                    if b > 0 and i > 0:
                        pe.wait_ge(rows_copied, 4 * b + i)
                    else:
                        pe.wait_ge(prep_copied, 4 * b + (KV + 1 if i else 4))
                    if b == 0 and s == 0:
                        pe.wait_ge(expanded0, 1)
                    else:
                        pe.wait_ge(expanded, 2 * b + s)
                    for j in range(4):
                        h = 8 * (i % 2) + 2 * j
                        pair = q_expand[:, s, h:h + 2, :].rearrange("p h c -> p (h c)")
                        mm = pe.transpose(out_ps[:, j * P:(j + 1) * P], pair, ident)
                mm.then_inc(prep_done, 1)

            def scores(n):
                b, k = ORDER[n]
                s = k // PER_TILE
                if n == FIRST_BLOCK[2 * b + s]:
                    pe.wait_ge(rows_copied, 4 * b + 2 * s + 2)
                    pe.wait_ge(prep_copied, 4 * b + KV + 1)
                    if n == 0:
                        pe.wait_ge(odd_copied, 2)
                        pe.wait_ge(heads0_ready, 1)
                    else:
                        pe.wait_ge(heads_ready, 2 * b + s)
                if n == 1:
                    pe.wait_ge(heads0_ready, 2)
                if n == 0:
                    pe.wait_ge(er_loaded, 32)
                    pe.wait_ge(mask_loaded, 16)
                if n >= 2:
                    pe.wait_ge(exp_done, n - 1)
                if n - 1 in FFN_AFTER:
                    pe.wait_ge(relu_done, E * (FFN_AFTER.index(n - 1) + 1))
                if n - 2 in FFN_AFTER:
                    pe.wait_ge(added, E * (FFN_AFTER.index(n - 2) + 1))
                keys = BLOCK * (k + 1)
                for g in range(GROUPS):
                    row0 = BLOCK * k + ROWS * g
                    seen = row0 + ROWS
                    group = (row0 - P * s) // ROWS
                    pe.matmul(sc[n % 2][:, g, 0:keys],
                              q_rows[:, b % 2, s, group, :, :].rearrange("p h r -> p (h r)"),
                              er_shift[:, S - 1 - row0:S - 1 - row0 + keys],
                              start=True, stop=False, skip_group_check=True)
                    mm = pe.matmul(sc[n % 2][:, g, 0:seen],
                                   q_heads[:, b % 2, s, group, :, :].rearrange("p h r -> p (h r)"),
                                   kT[:, b, 0:seen], start=False, stop=True, skip_group_check=True)
                mm.then_inc(scores_done, 1)

            def turn(n):
                pe.wait_ge(exp_done, n + 1)
                for c, key0, keys in units_of(n):
                    unit = UNITS_BEFORE[n] + c
                    if unit >= 2:
                        pe.wait_ge(turned_copied, unit - 1)
                    elif unit == 1:
                        pe.wait_ge(rows_copied, 4)
                    for g in range(GROUPS):
                        mm = pe.transpose(pt[unit % 2][0:keys, g * P:(g + 1) * P],
                                          probs[:, n % 3, g, key0:key0 + keys], ident)
                    mm.then_inc(turned, 1)

            def values(u):
                b, s = divmod(u, 2)
                pe.wait_ge(turned_copied, UNITS_BEFORE[LAST_BLOCK[u] + 1])
                if u == 0:
                    pe.wait_ge(filled, 5)
                elif s == 0:
                    pe.wait_ge(tile_copied, 3 * b)
                else:
                    pe.wait_ge(pv_copied, u)
                pe.wait_ge(prep_copied, 4 * b + KV + 1)
                for m in range(H // 4):
                    for c in range(s + 1):
                        for q in range(4):
                            mm = pe.matmul(tile_ps[VW * q:VW * (q + 1), P * m:P * (m + 1)],
                                           v_one[:, 2 * b + c, 4 * m + q, :], probsT[:, s + c, 4 * m + q, :],
                                           start=(c == 0), stop=(c == s), tile_position=(0, VW * q))
                mm.then_inc(pv_done, 1)

            def tile(j, step, u):
                last = JOBS[j][-1]
                if step == VALUES_T:
                    pe.wait_ge(pv_copied, last + 1)
                    if u > JOBS[j][0]:
                        pe.wait_ge(pv_used, u)
                    for m in range(H // 4):
                        mm = pe.transpose(tile_ps[:, P * m:P * (m + 1)], pv_sb[:, u % 2, m, :], ident)
                elif step == LN2_T:
                    pe.wait_ge(pv_used, last + 1)
                    pe.wait_ge(xn2_ready, j + 1)
                    for i in range(len(JOBS[j])):
                        mm = pe.transpose(tile_ps[:, P * i:P * (i + 1)], xn2[:, i, :], ident)
                elif step == GATE:
                    pe.wait_ge(tile_copied, 3 * j + 1)
                    pe.wait_ge(ffn_loaded, 80)
                    for i, u in enumerate(JOBS[j]):
                        mm = pe.matmul(tile_ps[:, E * i:E * (i + 1)], xn2T[:, u, :], gate_sb[:, :],
                                       start=True, stop=True)
                else:
                    pe.wait_ge(tile_copied, 3 * j + 2)
                    pe.wait_ge(gates_ready, j + 1)
                    for i, u in enumerate(JOBS[j]):
                        mm = pe.transpose(tile_ps[0:E, P * i:P * (i + 1)], gates[:, u, :], ident)
                mm.then_inc(tile_done, 1)

            def bias2(b):
                pe.wait_ge(tile_copied, 3 * (b + 1))
                pe.wait_ge(added, E * b)
                for s in range(2):
                    mm = pe.matmul(o_ps[1][:, s, :], gatesT[:, 2 * b + s, :], b2_sb[:, :],
                                   start=True, stop=True)
                mm.then_inc(bias2_done, 1)

            def hidden(b, e):
                i = E * b + e
                if e == 0:
                    pe.wait_ge(tile_copied, 3 * b + 1)
                    if b == B - 2:
                        pe.wait_ge(exp_done, BLOCKS - 1)
                if i >= 2:
                    pe.wait_ge(relu_done, i - 1)
                tok = xn2T[:, 2 * b:2 * b + 2, :].rearrange("p t n -> p (t n)")
                for c in range(2):
                    mm = pe.matmul(h_ps[i % 2][:, c, :], w1[:, e, P * c:P * (c + 1)], tok, start=True, stop=True)
                mm.then_inc(h_done, 1)

            def expert(b, e):
                i = E * b + e
                pe.wait_ge(relu_done, i + 1)
                if e == 0:
                    pe.wait_ge(exp_done, min(FFN_AFTER[b] + 1 if b < len(FFN_AFTER) else BLOCKS, BLOCKS))
                if e == 1:
                    pe.wait_ge(bias2_added, b + 1)
                if i >= 2:
                    pe.wait_ge(added, i - 1)
                for s in range(2):
                    for c in range(2):
                        mm = pe.matmul(o_ps[i % 2][:, s, :], hT[:, i % HT_BUFS, c, s * P:(s + 1) * P],
                                       w2[:, 2 * e + c, :], start=(c == 0), stop=(c == 1))
                mm.then_inc(expert_done, 1)

            def ffn(b, n):
                hidden(b, 0)
                hidden(b, 1)
                turn(n)
                expert(b, 0)
                bias2(b)
                for e in range(1, E):
                    if e + 1 < E:
                        hidden(b, e + 1)
                    expert(b, e)

            def keep_clock(count):
                for _ in range(count):
                    pe.matmul(sc[0][:, 0:2, :].rearrange("p g n -> p (g n)"), zeros[:, 0:P], zeros[:, P:],
                              start=True, stop=True)

            pe.wait_ge(zeroed, 1)
            keep_clock(WARM[0])
            for step in range(ROWS_2):
                prep(0, step)
                keep_clock(WARM[1 + step])
            for n in range(BLOCKS):
                scores(n)
                if n == 0:
                    prep(0, ROWS_2)
                    prep(0, ROWS_3)
                for b, step in PREP_AT[n]:
                    if step < ROWS_0:
                        prep(b, step)
                if n in VALUES_AT:
                    values(VALUES_AT[n])
                for j, step, u in TILE_AT[n]:
                    if n not in VALUES_AT:
                        tile(j, step, u)
                if n >= LAG and n - LAG not in FFN_AFTER:
                    turn(n - LAG)
                for b, step in PREP_AT[n]:
                    if step >= ROWS_0:
                        prep(b, step)
                for j, step, u in TILE_AT[n]:
                    if n in VALUES_AT:
                        tile(j, step, u)
                if n in FFN_AFTER:
                    ffn(FFN_AFTER.index(n), n)
            b, j = B - 2, B - 1
            hidden(b, 0)
            values(TILES - 2)
            hidden(b, 1)
            turn(BLOCKS - 1)
            expert(b, 0)
            bias2(b)
            values(TILES - 1)
            hidden(b, 2)
            expert(b, 1)
            tile(j, VALUES_T, TILES - 2)
            hidden(b, 3)
            expert(b, 2)
            tile(j, VALUES_T, TILES - 1)
            hidden(b, 4)
            expert(b, 3)
            hidden(b, 5)
            expert(b, 4)
            tile(j, LN2_T, None)
            hidden(b, 6)
            expert(b, 5)
            tile(j, GATE, None)
            hidden(b, 7)
            expert(b, 6)
            hidden(b + 1, 0)
            expert(b, 7)
            hidden(b + 1, 1)
            tile(j, GATE_T, None)
            expert(b + 1, 0)
            bias2(b + 1)
            for e in range(1, E):
                if e + 1 < E:
                    hidden(b + 1, e + 1)
                expert(b + 1, e)

        @block.scalar
        def _(act):
            act.dma_start(wide[:, :], t["const_wide"]).then_inc(const_loaded, 16)
            act.dma_start(wkT[:, :], t["wkT"]).then_inc(kv_loaded, 16)
            act.dma_start(wvT[:, :], t["wvT"]).then_inc(kv_loaded, 16)
            act.dma_start(bq_all[:, :], t["bq"].partition_broadcast(P)).then_inc(bias_loaded, 16)
            act.dma_start(bv_all[:, :], t["bv"].partition_broadcast(P)).then_inc(bias_loaded, 16)
            act.dma_start(bk_col[:, :], t["bk"]).then_inc(bias_loaded, 16)
            act.dma_start(q_rows[ROWS * DH:K_ROWS, :, :, :, :, :].rearrange("p a s g h r -> p (a s g) (h r)"),
                          t["const_rows"].unsqueeze(1).to_broadcast([ROWS, 4 * P // ROWS, P])
                          ).then_inc(mask_loaded, 16)

            def rows_out(b, i):
                act.wait_ge(prep_done, 8 * b + ROWS_0 + i + 1)
                s, h0 = i // 2, 8 * (i % 2)
                src = prep_bank(b, ROWS_0 + i)[:, :].rearrange("p (j g r) -> p j g r", j=4, r=ROWS)
                dst = q_rows[:, b % 2, s, :, h0:h0 + 8, :].rearrange("p g (j o) r -> p o j g r", o=2)
                last = act.activation(dst[0:64, 0, :, :, :], src[0:64, :, :, :], ACT.Copy)
                if b or s:
                    last = act.activation(dst[0:64, 1, :, :, :], src[64:128, :, :, :], ACT.Copy)
                last.then_inc(rows_copied, 1)

            def exponents(n):
                act.wait_ge(max_ready, n + 1)
                if n >= 3:
                    act.wait_ge(turned, UNITS_BEFORE[n - 2])
                keys = BLOCK * (ORDER[n][1] + 1)
                for g in range(GROUPS):
                    last = act.activation(probs[:, n % 3, g, 0:keys], sc[n % 2][:, g, 0:keys], ACT.Exp,
                                          bias=neg_max[:, n % 4, g:g + 1])
                last.then_inc(exp_done, 1)

            def values_out(u):
                act.wait_ge(pv_done, u + 1)
                act.activation(pv_sb[:, u % 2, :, :].rearrange("p m n -> p (m n)"), tile_ps[:, :], ACT.Copy
                               ).then_inc(pv_copied, 1)

            def gate_exponents(j):
                act.wait_ge(top_ready, j + 1)
                for i in range(len(JOBS[j])):
                    last = act.activation(gate_exp[:, i, :], logits[:, i, :], ACT.Exp, bias=neg_top[:, i:i + 1],
                                          accum_out=gate_sum[:, i:i + 1])
                last.then_inc(gate_exp_ready, 1)

            def relu(b, e):
                i = E * b + e
                act.wait_ge(h_done, i + 1)
                if i >= HT_BUFS:
                    act.wait_ge(expert_done, i - HT_BUFS + 1)
                if i == 0:
                    act.wait_ge(ffn_loaded, 80)
                for c in range(2):
                    last = act.activation(hT[:, i % HT_BUFS, c, :], h_ps[i % 2][:, c, :], ACT.Relu,
                                          bias=b1_col[:, 2 * e + c:2 * e + c + 1])
                last.then_inc(relu_done, 1)

            rows_out(0, 0)
            rows_out(0, 1)
            for n in range(BLOCKS):
                exponents(n)
                if n in VALUES_AT:
                    values_out(VALUES_AT[n])
                if n == 0:
                    rows_out(0, 2)
                    rows_out(0, 3)
                for b, step in PREP_AT[n]:
                    if step >= ROWS_0:
                        rows_out(b, step - ROWS_0)
                for j, step, u in TILE_AT[n]:
                    if step == GATE:
                        gate_exponents(j)
                if n in FFN_AFTER:
                    for e in range(E):
                        relu(FFN_AFTER.index(n), e)
            b = B - 2
            relu(b, 0)
            values_out(TILES - 2)
            relu(b, 1)
            values_out(TILES - 1)
            for e in range(2, 7):
                relu(b, e)
            gate_exponents(B - 1)
            for e in range(7, E):
                relu(b, e)
            for e in range(E):
                relu(b + 1, e)

        @block.vector
        def _(dve):
            chain = [0]

            def link(ins):
                chain[0] += 1
                ins.then_inc(dve_chain, 1)
                dve.wait_ge(dve_chain, chain[0])

            def prep_out(b, step):
                dve.wait_ge(prep_done, 8 * b + step + 1)
                src = prep_bank(b, step)
                if step == LN_T:
                    dve.tensor_copy(xnT[:, :], src[:, 0:S]).then_inc(prep_copied, 1)
                elif step == KV:
                    dve.tensor_scalar(kT[:, b, :], src[:, 0:S], bk_col[:, 0:1], None, ALU.add)
                    bv = bv_all[:, :].rearrange("p (h d) -> p h d", h=H).unsqueeze(1).to_broadcast([P, 2, H, DH])
                    dve.tensor_tensor(v_one[:, 2 * b:2 * b + 2, :, 0:DH],
                                      src[:, S:2 * S].rearrange("p (s h d) -> p s h d", s=2, h=H),
                                      bv, ALU.add).then_inc(prep_copied, 1)
                elif step == Q:
                    dve.scalar_tensor_tensor(out=q_sb[:, :, :], in0=src[:, 0:S].rearrange("p (s d) -> p s d", s=2),
                                             scalar=SCALE, in1=bq_scaled[:, :].unsqueeze(1).to_broadcast([P, 2, D]),
                                             op0=ALU.mult, op1=ALU.add).then_inc(prep_copied, 1)
                elif step == Q_T:
                    if b:
                        dve.wait_ge(heads_ready, 2 * b - 1)
                    dve.tensor_copy(qT[:, :, :].rearrange("p s n -> p (s n)"), src[:, 0:S]
                                    ).then_inc(prep_copied, 1)

            def expand0():
                dve.wait_ge(prep_copied, Q + 1)
                dve.tensor_tensor(
                    q_expand[:, 0, :, :].rearrange("p h (r d) -> p h r d", r=ROWS),
                    q_sb[:, 0, :].rearrange("p (h d) -> p h d", h=H).unsqueeze(2).to_broadcast([P, H, ROWS, DH]),
                    row_mask.unsqueeze(1).unsqueeze(3).to_broadcast([P, H, ROWS, DH]),
                    ALU.mult).then_inc(expanded0, 1)

            def odd_rows(i):
                dve.wait_ge(prep_done, ROWS_0 + i + 1)
                src = prep_bank(0, ROWS_0 + i)[:, :].rearrange("p (j g r) -> p j g r", j=4, r=ROWS)
                dst = q_rows[:, 0, 0, :, 8 * i:8 * i + 8, :].rearrange("p g (j o) r -> p o j g r", o=2)
                dve.tensor_copy(dst[0:64, 1, :, :, :], src[64:128, :, :, :]).then_inc(odd_copied, 1)

            def heads0(g0, g1):
                dve.wait_ge(prep_copied, 4)
                dve.tensor_tensor(
                    q_heads[:, 0, 0, g0:g1, :, :],
                    qT[:, 0, ROWS * g0:ROWS * g1].rearrange("p (g r) -> p g r", r=ROWS).unsqueeze(2)
                    .to_broadcast([P, g1 - g0, H, ROWS]),
                    head_mask.unsqueeze(1).unsqueeze(3).to_broadcast([P, g1 - g0, H, ROWS]),
                    ALU.mult).then_inc(heads0_ready, 1)

            def maxima(n):
                dve.wait_ge(scores_done, n + 1)
                keys = BLOCK * (ORDER[n][1] + 1)
                dve.tensor_reduce(neg_max[:, n % 4, :], sc[n % 2][:, :, 0:keys], AX.X, ALU.max,
                                  negate=True).then_inc(max_ready, 1)

            def turned_out(n):
                k = ORDER[n][1]
                u = TILE_OF[n]
                if u >= 2 and n == FIRST_BLOCK[u]:
                    dve.wait_ge(pv_done, u - 1)
                q0 = BLOCK * (k % PER_TILE)
                for c, key0, keys in units_of(n):
                    unit = UNITS_BEFORE[n] + c
                    dve.wait_ge(turned, unit + 1)
                    if n == 0:
                        dve.wait_ge(filled, 5)
                    dst = probsT[0:keys, k // PER_TILE + c, :, q0:q0 + BLOCK]
                    dve.tensor_copy(dst.rearrange("p h (g r) -> p g h r", g=GROUPS),
                                    pt[unit % 2][0:keys, :].rearrange("p (g h r) -> p g h r", g=GROUPS, h=H)
                                    ).then_inc(turned_copied, 1)

            def residual(j, u):
                i = JOBS[j].index(u)
                pv = tile_ps[:, :].rearrange("p (h c) -> p h c", h=H)
                link(dve.reciprocal(inv_sum[:, :], pv[:, :, DH]))
                dve.tensor_tensor(attn[:, :, :], pv[:, :, 0:DH],
                                  inv_sum[:, :].unsqueeze(2).to_broadcast([P, H, DH]), ALU.mult).then_inc(pv_used, 1)
                dve.wait_ge(pv_used, u + 1)
                link(dve.tensor_tensor(x1[:, u, :], attn[:, :, :].rearrange("p h d -> p (h d)"), x_sb[:, u, :],
                                       ALU.add))
                link(dve.bn_stats(stats2[:, i, :], x1[:, u, :]))
                link(dve.bn_aggr(mean_var2[:, i, :], stats2[:, i, :]))
                if u == JOBS[j][-1]:
                    dve.tensor_scalar(var_eps2[:, 0:i + 1], mean_var2[:, 0:i + 1, 1], EPS, None, ALU.add
                                      ).then_inc(var2_ready, 1)

            def norm2(j):
                dve.wait_ge(rstd2_ready, j + 1)
                if j:
                    dve.wait_ge(tile_done, tile_count(j - 1, LN2_T))
                for i, u in enumerate(JOBS[j]):
                    last = dve.tensor_scalar(xn2[:, i, :], x1[:, u, :], mean_var2[:, i, 0:1], rstd2[:, i:i + 1],
                                             ALU.subtract, ALU.mult)
                last.then_inc(xn2_ready, 1)

            def tile_out(j, step, u):
                dve.wait_ge(tile_done, tile_count(j, step, u))
                u0, w = JOBS[j][0], len(JOBS[j])
                if step == VALUES_T:
                    residual(j, u)
                elif step == LN2_T:
                    dve.tensor_copy(xn2T[:, u0:u0 + w, :].rearrange("p t n -> p (t n)"), tile_ps[:, 0:w * P]
                                    ).then_inc(tile_copied, 1)
                elif step == GATE:
                    dve.tensor_copy(logits[:, 0:w, :].rearrange("p t e -> p (t e)"), tile_ps[:, 0:w * E]
                                    ).then_inc(tile_copied, 1)
                    dve.wait_ge(tile_copied, 3 * j + 2)
                    for i in range(w):
                        last = dve.max(sorted8[:, i, :], logits[:, i, :])
                    link(last)
                    dve.tensor_scalar(neg_top[:, 0:w], sorted8[:, 0:w, 0], -1.0, None, ALU.mult
                                      ).then_inc(top_ready, 1)
                else:
                    dve.tensor_copy(gatesT[:, u0:u0 + w, :].rearrange("p t n -> p (t n)"), tile_ps[0:E, 0:w * P]
                                    ).then_inc(tile_copied, 1)

            def add_bias2(b):
                dve.wait_ge(bias2_done, b + 1)
                dve.wait_ge(added, E * b + 1)
                dve.tensor_tensor(x1[:, 2 * b:2 * b + 2, :], o_ps[1], x1[:, 2 * b:2 * b + 2, :], ALU.add
                                  ).then_inc(bias2_added, 1)

            def pick(j):
                u0, w = JOBS[j][0], len(JOBS[j])
                square = [P, w, E, E]
                link(dve.tensor_tensor(diff[:, 0:w], logits[:, 0:w, :].unsqueeze(2).to_broadcast(square),
                                       logits[:, 0:w, :].unsqueeze(3).to_broadcast(square), ALU.subtract))
                link(dve.scalar_tensor_tensor(out=above[:, 0:w], in0=diff[:, 0:w], scalar=-1.0,
                                              in1=tie_tri.unsqueeze(1).to_broadcast(square),
                                              op0=ALU.mult, op1=ALU.is_lt))
                link(dve.tensor_reduce(rank[:, 0:w, :], above[:, 0:w], AX.X, ALU.add))
                dve.wait_ge(gate_exp_ready, j + 1)
                for i in range(w):
                    dve.scalar_tensor_tensor(out=picked[:, i, :], in0=rank[:, i, :], scalar=2.0,
                                             in1=gate_exp[:, i, :], op0=ALU.is_lt, op1=ALU.mult,
                                             accum_out=picked_sum[:, i:i + 1])
                link(dve.reciprocal(inv_gate_sum[:, 0:w], gate_sum[:, 0:w]))
                link(dve.tensor_tensor(denom[:, 0:w], picked_sum[:, 0:w], inv_gate_sum[:, 0:w], ALU.mult))
                link(dve.tensor_scalar(guarded[:, 0:w], denom[:, 0:w], 1e-12, None, ALU.max))
                link(dve.reciprocal(inv_denom[:, 0:w], guarded[:, 0:w]))
                for i in range(w):
                    last = dve.tensor_scalar(gates[:, u0 + i, :], picked[:, i, :], inv_gate_sum[:, i:i + 1],
                                             inv_denom[:, i:i + 1], ALU.mult, ALU.mult)
                last.then_inc(gates_ready, 1)

            def add_expert(b, e):
                i = E * b + e
                dve.wait_ge(expert_done, i + 1)
                if e == 0:
                    dve.wait_ge(gates_ready, b + 1)
                elif e == 1:
                    dve.wait_ge(bias2_added, b + 1)
                else:
                    dve.wait_ge(added, i)
                for s in range(2):
                    u = 2 * b + s
                    last = dve.scalar_tensor_tensor(out=x1[:, u, :], in0=o_ps[i % 2][:, s, :],
                                                    scalar=gates[:, u, e:e + 1], in1=x1[:, u, :],
                                                    op0=ALU.mult, op1=ALU.add)
                last.then_inc(added, 1)

            def variances(u0, u1):
                for u in range(u0, u1):
                    ins = dve.bn_stats(stats[:, u, :], x_sb[:, u, :])
                link(ins)
                for u in range(u0, u1):
                    ins = dve.bn_aggr(mean_var[:, u, :], stats[:, u, :])
                link(ins)
                dve.tensor_scalar(var_eps[:, u0:u1], mean_var[:, u0:u1, 1], EPS, None, ALU.add
                                  ).then_inc(var_ready, 1)

            def norm1(u0, u1):
                for u in range(u0, u1):
                    dve.tensor_scalar(xn[:, u, :], x_sb[:, u, :], mean_var[:, u, 0:1], rstd[:, u:u + 1],
                                      ALU.subtract, ALU.mult).then_inc(xn_ready, 1)

            dve.wait_ge(x_loaded, 16)
            variances(0, 2)
            dve.wait_ge(rstd_ready, 1)
            norm1(0, 2)
            dve.wait_ge(bias_loaded, 48)
            prep_out(0, KV)
            dve.tensor_scalar(bq_scaled[:, :], bq_all[:, :], SCALE, None, ALU.mult).then_inc(bq_ready, 1)
            prep_out(0, LN_T)
            dve.wait_ge(bq_ready, 1)
            prep_out(0, Q)
            dve.wait_ge(const_loaded, 16)
            expand0()
            prep_out(0, Q_T)
            heads0(0, GROUPS)
            odd_rows(0)
            odd_rows(1)
            heads0(GROUPS, P // ROWS)
            for n in range(BLOCKS):
                maxima(n)
                if n == 0:
                    dve.wait_ge(rest_loaded, 32)
                    variances(2, TILES)
                if n % PER_BATCH == PER_BATCH - 2 and n // PER_BATCH + 2 < B:
                    norm1(2 * (n // PER_BATCH + 2), 2 * (n // PER_BATCH + 3))
                for b, step in PREP_AT[n]:
                    if step < ROWS_0:
                        prep_out(b, step)
                if n == 0:
                    dve.wait_ge(rstd_ready, 2)
                    norm1(2, 4)
                for j, step, u in TILE_AT[n]:
                    if n not in VALUES_AT:
                        tile_out(j, step, u)
                if n >= LAG and n - LAG not in FFN_AFTER:
                    turned_out(n - LAG)
                for j, step, u in TILE_AT[n]:
                    if n in VALUES_AT:
                        tile_out(j, step, u)
                    elif step == VALUES_T:
                        norm2(j)
                    elif step == GATE:
                        pick(j)
                if n in FFN_AFTER:
                    b = FFN_AFTER.index(n)
                    turned_out(n)
                    add_expert(b, 0)
                    add_bias2(b)
                    for e in range(1, E):
                        add_expert(b, e)
            b, j = B - 2, B - 1
            turned_out(BLOCKS - 1)
            add_expert(b, 0)
            add_bias2(b)
            add_expert(b, 1)
            tile_out(j, VALUES_T, TILES - 2)
            add_expert(b, 2)
            tile_out(j, VALUES_T, TILES - 1)
            add_expert(b, 3)
            norm2(j)
            add_expert(b, 4)
            tile_out(j, LN2_T, None)
            add_expert(b, 5)
            tile_out(j, GATE, None)
            add_expert(b, 6)
            pick(j)
            add_expert(b, 7)
            tile_out(j, GATE_T, None)
            add_expert(b + 1, 0)
            add_bias2(b + 1)
            for e in range(1, E):
                add_expert(b + 1, e)


def kernel(x, ctx_1024, L0_xattn_Wq, L0_xattn_bq, L0_xattn_Wk, L0_xattn_bk, L0_xattn_Wv, L0_xattn_bv,
           L0_xattn_Er, L0_ffn_gate, L0_ffn_W1, L0_ffn_b1, L0_ffn_W2, L0_ffn_b2):
    import concourse.bacc as bacc
    from concourse.bass_utils import run_bass_kernel_spmd

    a = lambda v: np.ascontiguousarray(np.asarray(v))
    arrays = {
        "x": a(x),
        "ctxT": a(np.asarray(ctx_1024).reshape(B * S, D).T),
        "wqT": a(np.asarray(L0_xattn_Wq).T),
        "wkT": a(np.asarray(L0_xattn_Wk).T),
        "wvT": a(np.asarray(L0_xattn_Wv).T),
        "bq": a(L0_xattn_bq).reshape(1, D),
        "bk": a(L0_xattn_bk).reshape(D, 1),
        "bv": a(L0_xattn_bv).reshape(1, D),
        "er_rows": np.concatenate([np.pad(np.asarray(L0_xattn_Er).T, ((0, 0), (r, BLOCK - r)))
                                   for r in range(ROWS)]),
        "gate": a(L0_ffn_gate),
        "w1": a(L0_ffn_W1),
        "b1T": a(np.asarray(L0_ffn_b1).reshape(CHUNKS, P).T),
        "w2": a(L0_ffn_W2),
        "b2": a(L0_ffn_b2),
    }
    arrays.update(shape_constants())
    nc = bacc.Bacc("TRN2", target_bir_lowering=False, num_devices=1)
    t = {k: nc.dram_tensor("in_" + k, v.shape, mybir.dt.from_np(v.dtype), kind="ExternalInput").ap()
         for k, v in arrays.items()}
    t["out"] = nc.dram_tensor("out", (B, S, D), F32, kind="ExternalOutput").ap()
    build(nc, t)
    r = run_bass_kernel_spmd(nc, [{"in_" + k: v for k, v in arrays.items()}], core_ids=[0])
    return r.results[0]["out"]
```

```python
from contextlib import ExitStack

import numpy as np

from concourse import mybir

F32 = mybir.dt.float32
BF16 = mybir.dt.bfloat16
ALU = mybir.AluOpType
ACT = mybir.ActivationFunctionType
AX = mybir.AxisListType

B, S, D, H, DH = 4, 256, 128, 16, 8
E, HID = 8, 256
P = 128
TILES = B * S // P
ROWS = 8
GROUPS = 4
BLOCK = ROWS * GROUPS
BLOCKS = B * S // BLOCK
PER_BATCH = S // BLOCK
PER_TILE = P // BLOCK
CHUNKS = 2 * E
HALF = H // 2
HP = HALF * DH
MASK_W = 2 * BLOCK - ROWS
MASKED = -1e30
EPS = 1e-5
SCALE = float(DH) ** -0.5
TIE = 1.2e-38
HT_BUFS = 3
PARTS_FROM = 3


def shape_constants():
    part = np.arange(P)
    row_mask = (part[:, None] % ROWS == np.arange(ROWS)).astype(np.float32)
    head_mask = (part[:, None] // DH == np.arange(H)).astype(np.float32)
    mask_rows = (np.arange(ROWS)[:, None] == np.tile(np.arange(ROWS), H)).astype(np.float32)
    after = np.arange(MASK_W)[None, :] - (BLOCK - ROWS) > np.arange(ROWS)[:, None]
    mask = np.concatenate([mask_rows, np.where(after, MASKED, 0.0).astype(np.float32)], axis=1)
    i, j = np.meshgrid(np.arange(E), np.arange(E), indexing="ij")
    tie = np.broadcast_to(np.where(j < i, TIE, 0.0).astype(np.float32).reshape(1, E * E), (P, E * E))
    wide = np.concatenate([np.eye(P, dtype=np.float32), row_mask, head_mask, tie], axis=1)
    return {"const_wide": np.ascontiguousarray(wide), "const_mask": mask}


def window(k, g):
    return GROUPS * BLOCK * k * (k + 1) // 2 + g * BLOCK * (k + 1)


WINDOWS = window(PER_BATCH, 0)


def er_windows(er):
    padded = [np.pad(er.T, ((0, 0), (r, BLOCK - r))) for r in range(ROWS)]
    shifted = np.concatenate(padded)
    cuts = []
    for k in range(PER_BATCH):
        for g in range(GROUPS):
            row0 = BLOCK * k + ROWS * g
            cuts.append(shifted[:, S - 1 - row0:S - 1 - row0 + BLOCK * (k + 1)])
    return np.ascontiguousarray(np.concatenate(cuts, axis=1))


MIXED = [0, 7, 1, 6, 2, 5, 3, 4]
ORDER = [(b, k) for b in range(B) for k in MIXED]
TILE_OF = [2 * b + k // PER_TILE for b, k in ORDER]
FIRST_BLOCK = [TILE_OF.index(u) for u in range(TILES)]
LAST_BLOCK = [max(n for n in range(BLOCKS) if TILE_OF[n] == u) for u in range(TILES)]

JOBS = [[2 * b, 2 * b + 1] for b in range(B)]


def units_of(n):
    keys = BLOCK * (ORDER[n][1] + 1)
    return [(c, c * P, min(P, keys - c * P)) for c in range((keys + P - 1) // P)]


def together(n):
    return {0: 4, 1: 2}.get(ORDER[n][1], 1)


def pitch(n):
    return BLOCK * (ORDER[n][1] + 1) if together(n) > 1 else S


LAG = 1
FFN_AFTER = [8 * b + 11 + 2 * LAG for b in range(B - 2)]

IN_PARTS = [k >= PARTS_FROM for _, k in ORDER]


def parts_count(n):
    return sum(IN_PARTS[:n + 1])


TURN_AT = {n: [] for n in range(BLOCKS)}
TURN_IN_FFN = {n: [] for n in FFN_AFTER + [BLOCKS - 1]}
for _n in range(BLOCKS):
    _in = [f for f in TURN_IN_FFN if _n <= f < _n + LAG]
    (TURN_IN_FFN[_in[0]] if _in else TURN_AT[_n + LAG]).append(_n)

UNITS_BEFORE = [0]
for _n in range(BLOCKS):
    UNITS_BEFORE.append(UNITS_BEFORE[-1] + len(units_of(_n)))


def by_act(n, c):
    return c == 1 or (n >= PER_BATCH and n % PER_BATCH == 1)


BY_ACT = [by_act(_n, c) for _n in range(BLOCKS) for c, _, _ in units_of(_n)]


def copies_count(unit, by_act):
    return sum(who == by_act for who in BY_ACT[:unit + 1])


KV, LN_T, Q, Q_T, ROWS_0, ROWS_1, ROWS_2, ROWS_3 = range(8)
VALUES_T, LN2_T, GATE = range(3)
VW = 32
WARM = (9, 2, 2, 0, 0, 0, 6, 4)

PREP_AT = [[(n // PER_BATCH + 1, n % PER_BATCH)] if n // PER_BATCH + 1 < B else [] for n in range(BLOCKS)]

VALUES_AT = {PER_BATCH * (_u // 2) + PER_BATCH - 1 + _u % 2 + LAG: _u for _u in range(TILES - 2)}
TILE_AT = [[] for n in range(BLOCKS)]
for _j in range(B - 1):
    for _i, _job_step in enumerate([(_j, VALUES_T, 2 * _j), (_j, VALUES_T, 2 * _j + 1), (_j, LN2_T, None),
                                    (_j, GATE, None)]):
        TILE_AT[PER_BATCH * (_j + 1) + LAG + _i].append(_job_step)


def done_count(b, step):
    return 8 * b + 1 + (step if b or step >= ROWS_0 else (LN_T, Q, Q_T, KV).index(step))


def copied_count(b, step):
    return done_count(b, step) - 4 * b


def tile_count(j, step, u=None):
    before = sum(len(tiles) + 2 for tiles in JOBS[:j])
    return before + (JOBS[j].index(u) + 1 if step == VALUES_T else len(JOBS[j]) + step)


def build(nc, t):
    ctx = ExitStack()
    with ctx:
        def sb(name, shape, dt=F32):
            return ctx.enter_context(nc.sbuf_tensor(name, shape, dt))

        def ps(name, shape, dt=F32):
            return ctx.enter_context(nc.psum_tensor(name, shape, dt))

        def sem(name):
            return ctx.enter_context(nc.semaphore(name))

        x_sb = sb("x_sb", [P, TILES, D])
        ctxT = sb("ctxT", [D, B * S])
        wqkv = sb("wqkv", [D, 3 * D + 1])
        wqT, wkT, wvT = (wqkv[:, i * D:(i + 1) * D] for i in range(3))
        bk_col = wqkv[:, 3 * D:3 * D + 1]
        bias_all = sb("bias_all", [P, 2, D])
        bq_all, bv_all = bias_all[:, 0, :], bias_all[:, 1, :]
        bq_scaled = sb("bq_scaled", [P, D])
        windows = sb("windows", [P, 2, WINDOWS])
        mask_sb = sb("mask_sb", [ROWS, P + MASK_W])
        mask_bf = sb("mask_bf", [ROWS, P + MASK_W], BF16)
        wide = sb("wide", [P, P + ROWS + H + E * E])
        ident = wide[:, 0:P]
        row_mask = wide[:, P:P + ROWS]
        head_mask = wide[:, P + ROWS:P + ROWS + H]
        tie_tri = wide[:, P + ROWS + H:].rearrange("p (i j) -> p i j", i=E)
        w1 = sb("w1", [D, E, HID])
        w2 = sb("w2", [P, CHUNKS, D])
        b1_col = sb("b1_col", [P, CHUNKS])
        b2_all = sb("b2_all", [P, E, D])
        gate_sb = sb("gate_sb", [D, E])

        stats = sb("stats", [P, TILES, 6])
        mean_var = sb("mean_var", [P, TILES, 2])
        var_eps = sb("var_eps", [P, TILES])
        rstd = sb("rstd", [P, TILES])
        minus_half = sb("minus_half", [P, TILES])
        xn = sb("xn", [P, TILES, D])
        xnT = sb("xnT", [D, S])
        kT = sb("kT", [D, B, S])
        v_one = sb("v_one", [P, TILES, H, VW])
        q_sb = sb("q_sb", [P, 2, D])
        qT = sb("qT", [D, 2, P])
        q_expand = sb("q_expand", [P, 2, HALF, 2, ROWS * DH])
        q_mix = sb("q_mix", [P, 2, 2, 2, P // ROWS, HALF, ROWS])
        neg_max = sb("neg_max", [P, 4, GROUPS])
        probs = sb("probs", [P, 3, GROUPS * S])
        probsT = sb("probsT", [P, 3, H, P])
        inv_sum = sb("inv_sum", [P, H])
        pv_sb = sb("pv_sb", [P, 2, H // 4, P])
        attn = sb("attn", [P, H, DH])
        x1 = sb("x1", [P, TILES, D])
        stats2 = sb("stats2", [P, 2, 6])
        mean_var2 = sb("mean_var2", [P, 2, 2])
        var_eps2 = sb("var_eps2", [P, 2])
        rstd2 = sb("rstd2", [P, 2])
        xn2 = sb("xn2", [P, 2, D])
        xn2T = sb("xn2T", [D, TILES, P])
        logits = sb("logits", [P, 2, E])
        sorted8 = sb("sorted8", [P, 2, E])
        neg_top = sb("neg_top", [P, 2])
        gate_exp = sb("gate_exp", [P, 2, E])
        gate_sum = sb("gate_sum", [P, 2])
        diff = sb("diff", [P, 2, E, E])
        above = sb("above", [P, 2, E, E])
        rank = sb("rank", [P, 2, E])
        picked = sb("picked", [P, 2, E])
        picked_sum = sb("picked_sum", [P, 2])
        inv_gate_sum = sb("inv_gate_sum", [P, 2])
        denom = sb("denom", [P, 2])
        guarded = sb("guarded", [P, 2])
        inv_denom = sb("inv_denom", [P, 2])
        gates = sb("gates", [P, TILES, E])
        zeros = sb("zeros", [P, P + 512], BF16)
        hT = sb("hT", [P, HT_BUFS, 2, S])

        sc = [ps(f"sc{i}", [P, GROUPS, S]) for i in range(2)]
        pt = [ps(f"pt{i}", [P, GROUPS * P]) for i in range(2)]
        tile_ps = ps("tile_ps", [P, 512])
        prep_ps = ps("prep_ps", [P, 512])
        h_ps = [sc[0][:, 2 * i:2 * i + 2, :] for i in range(2)]
        o_ps = [sc[1][:, 2 * i, :].rearrange("p (s d) -> p s d", d=D) for i in range(2)]

        def prep_bank(b, step):
            if b:
                return prep_ps
            return {KV: tile_ps, LN_T: prep_ps, Q: pt[0], Q_T: pt[1],
                    ROWS_0: sc[1][:, 0:2, :].rearrange("p g n -> p (g n)"),
                    ROWS_1: sc[1][:, 2:4, :].rearrange("p g n -> p (g n)"),
                    ROWS_2: tile_ps, ROWS_3: pt[1]}[step]

        def turned_operands(n, c):
            k = ORDER[n][1]
            q0 = BLOCK * (k % PER_TILE)
            keys = units_of(n)[c][2]
            bank = pt[(UNITS_BEFORE[n] + c) % 2]
            m = together(n)
            out = probsT[0:keys, k // PER_TILE + c, :, q0:q0 + BLOCK].rearrange("p h (g r) -> p g h r", r=ROWS)
            return [(out[:, j::m, :, :],
                     bank[j * keys:(j + 1) * keys, 0:GROUPS // m * P].rearrange("p (g h r) -> p g h r", h=H, r=ROWS))
                    for j in range(m)]

        def expand_operands(s, half):
            shape = [P, HALF, ROWS, DH]
            q = q_sb[:, s, half * HP:(half + 1) * HP].rearrange("p (h d) -> p h d", d=DH)
            return (q_expand[:, s, :, 1 - half, :].rearrange("p h (r d) -> p h r d", r=ROWS),
                    q.unsqueeze(2).to_broadcast(shape), row_mask.unsqueeze(1).unsqueeze(3).to_broadcast(shape))

        def heads_operands(b, s, half, g0, g1):
            rows = slice(HP * half, HP * (half + 1))
            shape = [HP, g1 - g0, HALF, ROWS]
            q = qT[rows, s, ROWS * g0:ROWS * g1].rearrange("p (g r) -> p g r", r=ROWS)
            mask = head_mask[rows, HALF * half:HALF * (half + 1)]
            return (q_mix[rows, b % 2, s, half, g0:g1, :, :], q.unsqueeze(2).to_broadcast(shape),
                    mask.unsqueeze(1).unsqueeze(3).to_broadcast(shape))

        def rows_operands(b, i, half):
            rows = slice(HP * (1 - half), HP * (2 - half))
            src = prep_bank(b, ROWS_0 + i)[rows, :].rearrange("p (h g r) -> p g h r", h=4, r=ROWS)
            h0 = 4 * (i % 2)
            return q_mix[rows, b % 2, i // 2, half, :, h0:h0 + 4, :], src

        def spread_operands(b, k, half):
            keys = BLOCK * (k + 1)
            rows = slice(HP * half, HP * (half + 1))
            out = windows[rows, half, window(k, 0):window(k + 1, 0)].rearrange("p (g n) -> p g n", g=GROUPS)
            return out, kT[rows, b, 0:keys].unsqueeze(1).to_broadcast([HP, GROUPS, keys])

        x_loaded = sem("x_loaded")
        rest_loaded = sem("rest_loaded")
        const_loaded = sem("const_loaded")
        er_loaded = sem("er_loaded")
        er7_loaded = sem("er7_loaded")
        er1_loaded = sem("er1_loaded")
        er_rest_loaded = sem("er_rest_loaded")
        mask_loaded = sem("mask_loaded")
        wqkv_loaded = sem("wqkv_loaded")
        ctx_loaded = sem("ctx_loaded")
        bias_loaded = sem("bias_loaded")
        ffn_loaded = sem("ffn_loaded")
        stored = sem("stored")
        zeroed = sem("zeroed")
        filled = sem("filled")
        bq_ready = sem("bq_ready")
        var_ready = sem("var_ready")
        rstd_ready = sem("rstd_ready")
        xn_ready = sem("xn_ready")
        prep_done = sem("prep_done")
        prep_copied = sem("prep_copied")
        rows_copied = sem("rows_copied")
        expanded0 = sem("expanded0")
        expanded = sem("expanded")
        mask_ready = sem("mask_ready")
        first_spread = sem("first_spread")
        spread = [sem(f"spread_{k}") for k in range(PER_BATCH)]
        k0_copied = sem("k0_copied")
        half2_copied = sem("half2_copied")
        heads0_ready = sem("heads0_ready")
        first_half_ready = sem("first_half_ready")
        heads_ready = sem("heads_ready")
        first_scored = sem("first_scored")
        first_max_ready = sem("first_max_ready")
        scores_done = sem("scores_done")
        max_ready = sem("max_ready")
        exp_done = sem("exp_done")
        turned = sem("turned")
        turned_copied = sem("turned_copied")
        act_copied = sem("act_copied")
        pv_done = sem("pv_done")
        pv_copied = sem("pv_copied")
        pv_used = sem("pv_used")
        var2_ready = sem("var2_ready")
        rstd2_ready = sem("rstd2_ready")
        xn2_ready = sem("xn2_ready")
        tile_done = sem("tile_done")
        tile_copied = sem("tile_copied")
        top_ready = sem("top_ready")
        gate_exp_ready = sem("gate_exp_ready")
        gates_ready = sem("gates_ready")
        h_done = sem("h_done")
        relu_done = sem("relu_done")
        expert_done = sem("expert_done")
        added = sem("added")
        dve_chain = sem("dve_chain")

        block = ctx.enter_context(nc.Block())

        @block.sync
        def _(sp):
            x_in = t["x"].rearrange("b (s p) d -> p (b s) d", p=P)
            out = t["out"].rearrange("b (s p) d -> p (b s) d", p=P)
            sp.dma_start(x_sb[:, 0:2, :], x_in[:, 0:2, :]).then_inc(x_loaded, 16)
            sp.dma_start(wqkv[:, :], t["wqkv"]).then_inc(wqkv_loaded, 16)

            def er_load(k0, k1, done):
                c0, c1 = window(k0, 0), window(k1, 0)
                sp.dma_start(windows[HP:P, 0, c0:c1], t["er"][:, c0:c1]).then_inc(done, 16)
                sp.dma_start(windows[0:HP, 1, c0:c1], t["er"][:, c0:c1]).then_inc(done, 16)

            def spread_keys(b, k):
                for half in range(2):
                    sp.dma_start(*spread_operands(b, k, half)).then_inc(spread[k], 16)

            def store(b):
                sp.wait_ge(added, E * (b + 1))
                sp.dma_start(out[:, 2 * b:2 * b + 2, :], x1[:, 2 * b:2 * b + 2, :]).then_inc(stored, 16)

            er_load(0, 1, er_loaded)
            er_load(7, 8, er7_loaded)
            er_load(1, 2, er1_loaded)
            sp.dma_start(x_sb[:, 2:TILES, :], x_in[:, 2:TILES, :]).then_inc(rest_loaded, 16)
            sp.wait_ge(k0_copied, 1)
            spread_keys(0, 7)
            spread_keys(0, 1)
            er_load(2, 7, er_rest_loaded)
            for _, k in ORDER[3:PER_BATCH]:
                spread_keys(0, k)
            sp.dma_start(w1[:, :, :], t["w1"].rearrange("e d h -> d e h")).then_inc(ffn_loaded, 16)
            sp.dma_start(w2[:, :, :], t["w2"].rearrange("e (c p) d -> p (e c) d", p=P)).then_inc(ffn_loaded, 16)
            sp.dma_start(b1_col[:, :], t["b1T"]).then_inc(ffn_loaded, 16)
            sp.dma_start(b2_all[:, :, :].rearrange("p e d -> p (e d)"), t["b2"].partition_broadcast(P)
                         ).then_inc(ffn_loaded, 16)
            sp.dma_start(gate_sb[:, :], t["gate"]).then_inc(ffn_loaded, 16)
            for n in range(BLOCKS - PER_BATCH):
                b, k = ORDER[n + PER_BATCH]
                sp.wait_ge(scores_done, n + 1)
                if n % PER_BATCH == 0:
                    sp.wait_ge(prep_copied, copied_count(b, KV))
                spread_keys(b, k)
                if n - 1 in FFN_AFTER:
                    store(FFN_AFTER.index(n - 1))
            for b in range(sum(at + 1 < BLOCKS - PER_BATCH for at in FFN_AFTER), B):
                store(b)
            sp.wait_ge(stored, 16 * B)

        @block.gpsimd
        def _(pool):
            pool.memset(zeros[:, :], 0.0).then_inc(zeroed, 1)
            pool.memset(minus_half[:, :], -0.5).then_inc(filled, 1)
            pool.memset(v_one[:, :, :, DH:DH + 1], 1.0).then_inc(filled, 1)
            pool.memset(v_one[:, :, :, DH + 1:VW], 0.0).then_inc(filled, 1)
            pool.wait_ge(filled, 3)
            pool.wait_ge(var_ready, 1)
            pool.tensor_tensor(rstd[:, 0:2], var_eps[:, 0:2], minus_half[:, 0:2], ALU.pow).then_inc(rstd_ready, 1)
            pool.memset(probsT[:, 0, :, :], 0.0).then_inc(filled, 1)
            pool.memset(probsT[:, 2, :, :], 0.0).then_inc(filled, 1)

            def expand(u):
                s = u % 2
                if s == 0 or u == 1:
                    pool.wait_ge(prep_copied, copied_count(u // 2, Q))
                if u >= 2:
                    pool.wait_ge(prep_done, 8 * (u // 2 - 1) + (ROWS_1 if s == 0 else ROWS_3) + 1)
                for half in range(2):
                    last = pool.tensor_tensor(*expand_operands(s, half), ALU.mult)
                last.then_inc(expanded, 1)

            def heads(b, s):
                pool.wait_ge(prep_copied, copied_count(b, Q_T))
                tiles = 2 * b + s
                pool.tensor_tensor(*heads_operands(b, s, 0, 0, P // ROWS), ALU.mult).then_inc(first_half_ready, 1)
                pool.wait_ge(first_half_ready, tiles)
                pool.tensor_tensor(*heads_operands(b, s, 1, 0, P // ROWS), ALU.mult).then_inc(heads_ready, 1)
                pool.wait_ge(heads_ready, tiles)

            def power(j):
                pool.wait_ge(var2_ready, j + 1)
                w = len(JOBS[j])
                pool.tensor_tensor(rstd2[:, 0:w], var_eps2[:, 0:w], minus_half[:, 0:w], ALU.pow
                                   ).then_inc(rstd2_ready, 1)

            pool.wait_ge(const_loaded, 16)
            expand(1)
            heads(0, 1)
            for i, (u0, u1) in enumerate(((2, 4), (4, TILES))):
                pool.wait_ge(var_ready, i + 2)
                pool.tensor_tensor(rstd[:, u0:u1], var_eps[:, u0:u1], minus_half[:, u0:u1], ALU.pow
                                   ).then_inc(rstd_ready, 1)
            for b in range(1, B):
                if b >= 2:
                    power(b - 2)
                expand(2 * b)
                heads(b, 0)
                expand(2 * b + 1)
                heads(b, 1)
            power(B - 2)
            power(B - 1)

        @block.tensor
        def _(pe):
            def prep(b, step):
                out_ps = prep_bank(b, step)
                if step == KV:
                    pe.wait_ge(ctx_loaded, 16)
                    pe.wait_ge(wqkv_loaded, 16)
                    if b > 1:
                        pe.wait_ge(rows_copied, 4 * b)
                    if b > 0:
                        pe.wait_ge(rest_loaded, 32)
                    pe.matmul(out_ps[:, 0:S], wkT[:, :], ctxT[:, b * S:(b + 1) * S], start=True, stop=True)
                    for s in range(2):
                        out = out_ps[:, S + s * P:S + (s + 1) * P]
                        mm = pe.matmul(out, ctxT[:, b * S + s * P:b * S + (s + 1) * P], wvT[:, :],
                                       start=True, stop=True)
                elif step == LN_T:
                    if b > 0:
                        pe.wait_ge(prep_copied, copied_count(b, KV))
                    else:
                        pe.wait_ge(const_loaded, 16)
                    pe.wait_ge(xn_ready, 2 * b + 2)
                    for s in range(2):
                        mm = pe.transpose(out_ps[:, s * P:(s + 1) * P], xn[:, 2 * b + s, :], ident)
                elif step == Q:
                    pe.wait_ge(prep_copied, copied_count(b, LN_T))
                    pe.wait_ge(wqkv_loaded, 16)
                    for s in range(2):
                        out = out_ps[:, s * P:(s + 1) * P]
                        mm = pe.matmul(out, xnT[:, s * P:(s + 1) * P], wqT[:, :], start=True, stop=True)
                elif step == Q_T:
                    pe.wait_ge(prep_copied, copied_count(b, Q))
                    for s in range(2):
                        mm = pe.transpose(out_ps[:, s * P:(s + 1) * P], q_sb[:, s, :], ident)
                else:
                    i = step - ROWS_0
                    s = i // 2
                    if b > 0 and i > 0:
                        pe.wait_ge(rows_copied, 4 * b + i)
                    elif b > 0:
                        pe.wait_ge(prep_copied, copied_count(b, Q_T))
                    elif i > 1:
                        pe.wait_ge(prep_copied, copied_count(0, KV))
                    if b == 0 and s == 0:
                        pe.wait_ge(expanded0, 1)
                    else:
                        pe.wait_ge(expanded, 2 * b + s)
                    for j in range(4):
                        pair = q_expand[:, s, 4 * (i % 2) + j, :, :].rearrange("p a c -> p (a c)")
                        mm = pe.transpose(out_ps[:, j * P:(j + 1) * P], pair, ident)
                mm.then_inc(prep_done, 1)

            def scores(n):
                b, k = ORDER[n]
                s = k // PER_TILE
                if n == FIRST_BLOCK[2 * b + s]:
                    pe.wait_ge(rows_copied, 4 * b + 2 * s + 2)
                    if b:
                        pe.wait_ge(prep_copied, copied_count(b, KV))
                    else:
                        pe.wait_ge(k0_copied, 1)
                    if n == 0:
                        pe.wait_ge(half2_copied, 1)
                        pe.wait_ge(heads0_ready, 1)
                    else:
                        pe.wait_ge(heads_ready, 2 * b + s)
                if n == 0:
                    pe.wait_ge(er_loaded, 32)
                    pe.wait_ge(mask_ready, 1)
                    pe.wait_ge(first_spread, 1)
                elif n == 1:
                    pe.wait_ge(half2_copied, 3)
                    pe.wait_ge(heads0_ready, 2)
                    pe.wait_ge(er7_loaded, 32)
                elif n == 2:
                    pe.wait_ge(er1_loaded, 32)
                elif n == 3:
                    pe.wait_ge(er_rest_loaded, 32)
                if n:
                    pe.wait_ge(spread[k], 32 * (b if k == ORDER[0][1] else b + 1))
                if n >= 2:
                    pe.wait_ge(exp_done, n - 1)
                if n - 1 in FFN_AFTER:
                    pe.wait_ge(relu_done, E * (FFN_AFTER.index(n - 1) + 1))
                if n - 2 in FFN_AFTER:
                    pe.wait_ge(added, E * (FFN_AFTER.index(n - 2) + 1))
                keys = BLOCK * (k + 1)
                for g in range(GROUPS):
                    row0 = BLOCK * k + ROWS * g
                    group = (row0 - P * s) // ROWS
                    for half in range(2):
                        pe.matmul(sc[n % 2][HP * half:HP * (half + 1), g, 0:keys],
                                  q_mix[:, b % 2, s, half, group, :, :].rearrange("p h r -> p (h r)"),
                                  windows[:, half, window(k, g):window(k, g) + keys],
                                  start=True, stop=False, tile_position=(0, HP * half), skip_group_check=True)
                    shift = P + BLOCK - ROWS - ROWS * g
                    mm = pe.matmul(sc[n % 2][:, g, keys - BLOCK:keys], mask_bf[:, 0:P],
                                   mask_bf[:, shift:shift + BLOCK], start=False, stop=True, skip_group_check=True)
                    if IN_PARTS[n] and g == 1:
                        mm.then_inc(first_scored, 1)
                mm.then_inc(scores_done, 1)

            def turn(n):
                pe.wait_ge(exp_done, n + 1)
                for c, key0, keys in units_of(n):
                    unit = UNITS_BEFORE[n] + c
                    if unit >= 2 and BY_ACT[unit - 2]:
                        pe.wait_ge(act_copied, copies_count(unit - 2, True))
                    elif unit >= 2:
                        pe.wait_ge(turned_copied, copies_count(unit - 2, False))
                    elif unit == 1:
                        pe.wait_ge(rows_copied, 4)
                        pe.wait_ge(half2_copied, 3)
                    m = together(n)
                    for i in range(GROUPS // m):
                        mm = pe.transpose(pt[unit % 2][0:m * keys, i * P:(i + 1) * P],
                                          probs[:, n % 3, m * i * pitch(n) + key0:m * i * pitch(n) + key0 + m * keys],
                                          ident)
                    mm.then_inc(turned, 1)

            def values(u):
                b, s = divmod(u, 2)
                last_unit = UNITS_BEFORE[LAST_BLOCK[u] + 1] - 1
                pe.wait_ge(turned_copied, copies_count(last_unit, False))
                if s:
                    pe.wait_ge(act_copied, copies_count(last_unit, True))
                if u == 0:
                    pe.wait_ge(filled, 5)
                elif s == 0:
                    pe.wait_ge(tile_copied, 2 * b)
                else:
                    pe.wait_ge(pv_copied, u)
                pe.wait_ge(prep_copied, copied_count(b, KV))
                for m in range(H // 4):
                    for c in range(s + 1):
                        for q in range(4):
                            mm = pe.matmul(tile_ps[VW * q:VW * (q + 1), P * m:P * (m + 1)],
                                           v_one[:, 2 * b + c, 4 * m + q, :], probsT[:, s + c, 4 * m + q, :],
                                           start=(c == 0), stop=(c == s), tile_position=(0, VW * q))
                mm.then_inc(pv_done, 1)

            def tile(j, step, u):
                last = JOBS[j][-1]
                if step == VALUES_T:
                    pe.wait_ge(pv_copied, last + 1)
                    if u > JOBS[j][0]:
                        pe.wait_ge(pv_used, u)
                    for m in range(H // 4):
                        mm = pe.transpose(tile_ps[:, P * m:P * (m + 1)], pv_sb[:, u % 2, m, :], ident)
                elif step == LN2_T:
                    pe.wait_ge(pv_used, last + 1)
                    pe.wait_ge(xn2_ready, j + 1)
                    for i in range(len(JOBS[j])):
                        mm = pe.transpose(tile_ps[:, P * i:P * (i + 1)], xn2[:, i, :], ident)
                elif step == GATE:
                    pe.wait_ge(tile_copied, 2 * j + 1)
                    pe.wait_ge(ffn_loaded, 80)
                    for i, u in enumerate(JOBS[j]):
                        mm = pe.matmul(tile_ps[:, E * i:E * (i + 1)], xn2T[:, u, :], gate_sb[:, :],
                                       start=True, stop=True)
                mm.then_inc(tile_done, 1)

            def hidden(b, e):
                i = E * b + e
                if e == 0:
                    pe.wait_ge(tile_copied, 2 * b + 1)
                    pe.wait_ge(exp_done, FFN_AFTER[b] if b < len(FFN_AFTER) else BLOCKS - 1)
                if i >= 2:
                    pe.wait_ge(relu_done, i - 1)
                tok = xn2T[:, 2 * b:2 * b + 2, :].rearrange("p t n -> p (t n)")
                for c in range(2):
                    mm = pe.matmul(h_ps[i % 2][:, c, :], w1[:, e, P * c:P * (c + 1)], tok, start=True, stop=True)
                mm.then_inc(h_done, 1)

            def expert(b, e):
                i = E * b + e
                pe.wait_ge(relu_done, i + 1)
                if e == 0:
                    pe.wait_ge(exp_done, min(FFN_AFTER[b] + 1 if b < len(FFN_AFTER) else BLOCKS, BLOCKS))
                if i >= 2:
                    pe.wait_ge(added, i - 1)
                for s in range(2):
                    for c in range(2):
                        mm = pe.matmul(o_ps[i % 2][:, s, :], hT[:, i % HT_BUFS, c, s * P:(s + 1) * P],
                                       w2[:, 2 * e + c, :], start=(c == 0), stop=(c == 1))
                mm.then_inc(expert_done, 1)

            def ffn(b, n):
                hidden(b, 0)
                hidden(b, 1)
                for m in TURN_IN_FFN[n]:
                    turn(m)
                expert(b, 0)
                for e in range(1, E):
                    if e + 1 < E:
                        hidden(b, e + 1)
                    expert(b, e)

            def keep_clock(count, bank=sc[0]):
                for _ in range(count):
                    pe.matmul(bank[:, 0:2, :].rearrange("p g n -> p (g n)"), zeros[:, 0:P], zeros[:, P:],
                              start=True, stop=True)

            pe.wait_ge(zeroed, 1)
            keep_clock(WARM[0])
            for i, step in enumerate((LN_T, Q, Q_T, KV, ROWS_0, ROWS_1)):
                prep(0, step)
                keep_clock(WARM[1 + i])
            for n in range(BLOCKS):
                scores(n)
                if n == 0:
                    prep(0, ROWS_2)
                    prep(0, ROWS_3)
                if n in VALUES_AT:
                    values(VALUES_AT[n])
                for b, step in PREP_AT[n]:
                    if step < ROWS_0:
                        prep(b, step)
                if n == 0:
                    keep_clock(WARM[-1], sc[1])
                for j, step, u in TILE_AT[n]:
                    if n not in VALUES_AT and step != LN2_T:
                        tile(j, step, u)
                for m in TURN_AT[n]:
                    turn(m)
                for b, step in PREP_AT[n]:
                    if step >= ROWS_0:
                        prep(b, step)
                for j, step, u in TILE_AT[n]:
                    if n in VALUES_AT or step == LN2_T:
                        tile(j, step, u)
                if n in FFN_AFTER:
                    ffn(FFN_AFTER.index(n), n)
            b, j = B - 2, B - 1
            hidden(b, 0)
            for n in TURN_IN_FFN[BLOCKS - 1][:-1]:
                turn(n)
            values(TILES - 2)
            hidden(b, 1)
            turn(BLOCKS - 1)
            expert(b, 0)
            values(TILES - 1)
            hidden(b, 2)
            expert(b, 1)
            tile(j, VALUES_T, TILES - 2)
            hidden(b, 3)
            expert(b, 2)
            tile(j, VALUES_T, TILES - 1)
            hidden(b, 4)
            expert(b, 3)
            hidden(b, 5)
            expert(b, 4)
            hidden(b, 6)
            tile(j, LN2_T, None)
            expert(b, 5)
            hidden(b, 7)
            tile(j, GATE, None)
            expert(b, 6)
            hidden(b + 1, 0)
            expert(b, 7)
            hidden(b + 1, 1)
            expert(b + 1, 0)
            for e in range(1, E):
                if e + 1 < E:
                    hidden(b + 1, e + 1)
                expert(b + 1, e)

        @block.scalar
        def _(act):
            act.dma_start(wide[:, :], t["const_wide"]).then_inc(const_loaded, 16)
            act.dma_start(bias_all[:, :, :].rearrange("p i d -> p (i d)"), t["bias"].partition_broadcast(P)
                          ).then_inc(bias_loaded, 16)
            act.dma_start(ctxT[:, 0:S], t["ctxT"][:, 0:S]).then_inc(ctx_loaded, 16)
            act.dma_start(mask_sb[:, :], t["const_mask"]).then_inc(mask_loaded, 16)
            act.dma_start(ctxT[:, S:B * S], t["ctxT"][:, S:B * S]).then_inc(rest_loaded, 16)

            def rows_out(b, i):
                act.wait_ge(prep_done, done_count(b, ROWS_0 + i))
                out, src = rows_operands(b, i, 0)
                last = act.activation(out, src, ACT.Copy)
                if b or i == 0:
                    out, src = rows_operands(b, i, 1)
                    last = act.activation(out, src, ACT.Copy)
                last.then_inc(rows_copied, 1)

            def act_out(n):
                for c, _, _ in units_of(n):
                    if by_act(n, c):
                        u = TILE_OF[n]
                        act.wait_ge(turned, UNITS_BEFORE[n] + c + 1)
                        if u >= 2 and n == FIRST_BLOCK[u]:
                            act.wait_ge(pv_done, u - 1)
                        if n == FIRST_BLOCK[1]:
                            act.wait_ge(filled, 5)
                        (out, src), = turned_operands(n, c)
                        act.activation(out, src, ACT.Copy).then_inc(act_copied, 1)

            def exponents(n):
                if IN_PARTS[n]:
                    act.wait_ge(first_max_ready, parts_count(n))
                else:
                    act.wait_ge(max_ready, n + 1)
                if n >= 3:
                    act.wait_ge(turned, UNITS_BEFORE[n - 2])
                keys = BLOCK * (ORDER[n][1] + 1)
                for g in range(GROUPS):
                    if g == 2:
                        for m in TURN_AT[n]:
                            act_out(m)
                    if g == 2 and VALUES_AT.get(n, 0) % 2:
                        values_out(VALUES_AT[n])
                    if g == 2 and IN_PARTS[n]:
                        act.wait_ge(max_ready, n + 1)
                    last = act.activation(probs[:, n % 3, g * pitch(n):g * pitch(n) + keys],
                                          sc[n % 2][:, g, 0:keys], ACT.Exp, bias=neg_max[:, n % 4, g:g + 1])
                last.then_inc(exp_done, 1)

            def values_out(u):
                act.wait_ge(pv_done, u + 1)
                act.activation(pv_sb[:, u % 2, :, :].rearrange("p m n -> p (m n)"), tile_ps[:, :], ACT.Copy
                               ).then_inc(pv_copied, 1)

            def gate_exponents(j):
                act.wait_ge(top_ready, j + 1)
                for i in range(len(JOBS[j])):
                    last = act.activation(gate_exp[:, i, :], logits[:, i, :], ACT.Exp, bias=neg_top[:, i:i + 1],
                                          accum_out=gate_sum[:, i:i + 1])
                last.then_inc(gate_exp_ready, 1)

            def relu(b, e):
                i = E * b + e
                act.wait_ge(h_done, i + 1)
                if i >= HT_BUFS:
                    act.wait_ge(expert_done, i - HT_BUFS + 1)
                if i == 0:
                    act.wait_ge(ffn_loaded, 80)
                for c in range(2):
                    last = act.activation(hT[:, i % HT_BUFS, c, :], h_ps[i % 2][:, c, :], ACT.Relu,
                                          bias=b1_col[:, 2 * e + c:2 * e + c + 1])
                last.then_inc(relu_done, 1)

            act.wait_ge(prep_done, done_count(0, KV))
            act.activation(kT[:, 0, :], prep_bank(0, KV)[:, 0:S], ACT.Identity, bias=bk_col
                           ).then_inc(k0_copied, 1)
            act.wait_ge(k0_copied, 1)
            for half in range(2):
                last = act.activation(*spread_operands(0, ORDER[0][1], half), ACT.Copy)
            last.then_inc(first_spread, 1)
            rows_out(0, 0)
            rows_out(0, 1)
            for n in range(BLOCKS):
                exponents(n)
                if VALUES_AT.get(n, 1) % 2 == 0:
                    values_out(VALUES_AT[n])
                if n == 0:
                    rows_out(0, 2)
                    rows_out(0, 3)
                if n in FFN_AFTER:
                    relu(FFN_AFTER.index(n), 0)
                for b, step in PREP_AT[n]:
                    if step >= ROWS_0:
                        rows_out(b, step - ROWS_0)
                for j, step, u in TILE_AT[n]:
                    if step == GATE:
                        gate_exponents(j)
                if n in FFN_AFTER:
                    relu(FFN_AFTER.index(n), 1)
                    for m in TURN_IN_FFN[n]:
                        act_out(m)
                    for e in range(2, E):
                        relu(FFN_AFTER.index(n), e)
            b = B - 2
            relu(b, 0)
            values_out(TILES - 2)
            relu(b, 1)
            for n in TURN_IN_FFN[BLOCKS - 1]:
                act_out(n)
            values_out(TILES - 1)
            for e in range(2, E):
                relu(b, e)
            gate_exponents(B - 1)
            for e in range(E):
                relu(b + 1, e)

        @block.vector
        def _(dve):
            chain = [0]

            def link(ins):
                chain[0] += 1
                ins.then_inc(dve_chain, 1)
                dve.wait_ge(dve_chain, chain[0])

            def prep_out(b, step):
                dve.wait_ge(prep_done, done_count(b, step))
                src = prep_bank(b, step)
                if step == LN_T:
                    dve.tensor_copy(xnT[:, :], src[:, 0:S]).then_inc(prep_copied, 1)
                elif step == KV:
                    if b:
                        dve.tensor_scalar(kT[:, b, :], src[:, 0:S], bk_col, None, ALU.add)
                    bv = bv_all.rearrange("p (h d) -> p h d", h=H).unsqueeze(1).to_broadcast([P, 2, H, DH])
                    dve.tensor_tensor(v_one[:, 2 * b:2 * b + 2, :, 0:DH],
                                      src[:, S:2 * S].rearrange("p (s h d) -> p s h d", s=2, h=H),
                                      bv, ALU.add).then_inc(prep_copied, 1)
                elif step == Q:
                    dve.scalar_tensor_tensor(out=q_sb[:, :, :], in0=src[:, 0:S].rearrange("p (s d) -> p s d", s=2),
                                             scalar=SCALE, in1=bq_scaled[:, :].unsqueeze(1).to_broadcast([P, 2, D]),
                                             op0=ALU.mult, op1=ALU.add).then_inc(prep_copied, 1)
                elif step == Q_T:
                    if b:
                        dve.wait_ge(heads_ready, 2 * b - 1)
                    dve.tensor_copy(qT[:, :, :].rearrange("p s n -> p (s n)"), src[:, 0:S]
                                    ).then_inc(prep_copied, 1)

            def expand0():
                dve.wait_ge(prep_copied, copied_count(0, Q))
                for half in range(2):
                    last = dve.tensor_tensor(*expand_operands(0, half), ALU.mult)
                last.then_inc(expanded0, 1)

            def second_half_rows(i):
                dve.wait_ge(prep_done, done_count(0, ROWS_0 + i))
                dve.tensor_copy(*rows_operands(0, i, 1)).then_inc(half2_copied, 1)

            def heads0(g0, g1):
                dve.wait_ge(prep_copied, copied_count(0, Q_T))
                for half in range(2):
                    last = dve.tensor_tensor(*heads_operands(0, 0, half, g0, g1), ALU.mult)
                last.then_inc(heads0_ready, 1)

            def maxima(n):
                keys = BLOCK * (ORDER[n][1] + 1)
                g0 = 0
                if IN_PARTS[n]:
                    dve.wait_ge(first_scored, parts_count(n))
                    dve.tensor_reduce(neg_max[:, n % 4, 0:2], sc[n % 2][:, 0:2, 0:keys], AX.X, ALU.max,
                                      negate=True).then_inc(first_max_ready, 1)
                    g0 = 2
                for j, step, u in TILE_AT[n]:
                    if step == LN2_T:
                        norm2(j)
                dve.wait_ge(scores_done, n + 1)
                dve.tensor_reduce(neg_max[:, n % 4, g0:], sc[n % 2][:, g0:, 0:keys], AX.X, ALU.max,
                                  negate=True).then_inc(max_ready, 1)

            def turned_out(n):
                if by_act(n, 0):
                    return
                u = TILE_OF[n]
                dve.wait_ge(turned, UNITS_BEFORE[n] + 1)
                if u >= 2 and n == FIRST_BLOCK[u]:
                    dve.wait_ge(pv_done, u - 1)
                if n == 0:
                    dve.wait_ge(filled, 5)
                for out, src in turned_operands(n, 0):
                    last = dve.tensor_copy(out, src)
                last.then_inc(turned_copied, 1)

            def residual(j, u):
                i = JOBS[j].index(u)
                pv = tile_ps[:, :].rearrange("p (h c) -> p h c", h=H)
                link(dve.reciprocal(inv_sum[:, :], pv[:, :, DH]))
                dve.tensor_tensor(attn[:, :, :], pv[:, :, 0:DH],
                                  inv_sum[:, :].unsqueeze(2).to_broadcast([P, H, DH]), ALU.mult).then_inc(pv_used, 1)
                dve.wait_ge(pv_used, u + 1)
                link(dve.tensor_tensor(x1[:, u, :], attn[:, :, :].rearrange("p h d -> p (h d)"), x_sb[:, u, :],
                                       ALU.add))
                link(dve.bn_stats(stats2[:, i, :], x1[:, u, :]))
                link(dve.bn_aggr(mean_var2[:, i, :], stats2[:, i, :]))
                if u == JOBS[j][-1]:
                    dve.tensor_scalar(var_eps2[:, 0:i + 1], mean_var2[:, 0:i + 1, 1], EPS, None, ALU.add
                                      ).then_inc(var2_ready, 1)

            def norm2(j):
                dve.wait_ge(rstd2_ready, j + 1)
                if j:
                    dve.wait_ge(tile_done, tile_count(j - 1, LN2_T))
                for i, u in enumerate(JOBS[j]):
                    last = dve.tensor_scalar(xn2[:, i, :], x1[:, u, :], mean_var2[:, i, 0:1], rstd2[:, i:i + 1],
                                             ALU.subtract, ALU.mult)
                last.then_inc(xn2_ready, 1)

            def tile_out(j, step, u):
                dve.wait_ge(tile_done, tile_count(j, step, u))
                u0, w = JOBS[j][0], len(JOBS[j])
                if step == VALUES_T:
                    residual(j, u)
                elif step == LN2_T:
                    dve.tensor_copy(xn2T[:, u0:u0 + w, :].rearrange("p t n -> p (t n)"), tile_ps[:, 0:w * P]
                                    ).then_inc(tile_copied, 1)
                elif step == GATE:
                    dve.tensor_copy(logits[:, 0:w, :].rearrange("p t e -> p (t e)"), tile_ps[:, 0:w * E]
                                    ).then_inc(tile_copied, 1)
                    dve.wait_ge(tile_copied, 2 * j + 2)
                    for i in range(w):
                        last = dve.max(sorted8[:, i, :], logits[:, i, :])
                    link(last)
                    dve.tensor_scalar(neg_top[:, 0:w], sorted8[:, 0:w, 0], -1.0, None, ALU.mult
                                      ).then_inc(top_ready, 1)

            def pick(j):
                u0, w = JOBS[j][0], len(JOBS[j])
                square = [P, w, E, E]
                link(dve.tensor_tensor(diff[:, 0:w], logits[:, 0:w, :].unsqueeze(2).to_broadcast(square),
                                       logits[:, 0:w, :].unsqueeze(3).to_broadcast(square), ALU.subtract))
                link(dve.scalar_tensor_tensor(out=above[:, 0:w], in0=diff[:, 0:w], scalar=-1.0,
                                              in1=tie_tri.unsqueeze(1).to_broadcast(square),
                                              op0=ALU.mult, op1=ALU.is_lt))
                link(dve.tensor_reduce(rank[:, 0:w, :], above[:, 0:w], AX.X, ALU.add))
                dve.wait_ge(gate_exp_ready, j + 1)
                for i in range(w):
                    dve.scalar_tensor_tensor(out=picked[:, i, :], in0=rank[:, i, :], scalar=2.0,
                                             in1=gate_exp[:, i, :], op0=ALU.is_lt, op1=ALU.mult,
                                             accum_out=picked_sum[:, i:i + 1])
                link(dve.reciprocal(inv_gate_sum[:, 0:w], gate_sum[:, 0:w]))
                link(dve.tensor_tensor(denom[:, 0:w], picked_sum[:, 0:w], inv_gate_sum[:, 0:w], ALU.mult))
                link(dve.tensor_scalar(guarded[:, 0:w], denom[:, 0:w], 1e-12, None, ALU.max))
                link(dve.reciprocal(inv_denom[:, 0:w], guarded[:, 0:w]))
                for i in range(w):
                    last = dve.tensor_scalar(gates[:, u0 + i, :], picked[:, i, :], inv_gate_sum[:, i:i + 1],
                                             inv_denom[:, i:i + 1], ALU.mult, ALU.mult)
                last.then_inc(gates_ready, 1)

            def add_expert(b, e):
                i = E * b + e
                if e == 0:
                    dve.wait_ge(gates_ready, b + 1)
                else:
                    dve.wait_ge(added, i)
                tiles = (2 * b, 2 * b + 1)
                for u in tiles:
                    last = dve.scalar_tensor_tensor(out=x1[:, u, :], in0=b2_all[:, e, :],
                                                    scalar=gates[:, u, e:e + 1], in1=x1[:, u, :],
                                                    op0=ALU.mult, op1=ALU.add)
                link(last)
                dve.wait_ge(expert_done, i + 1)
                for s, u in enumerate(tiles):
                    last = dve.scalar_tensor_tensor(out=x1[:, u, :], in0=o_ps[i % 2][:, s, :],
                                                    scalar=gates[:, u, e:e + 1], in1=x1[:, u, :],
                                                    op0=ALU.mult, op1=ALU.add)
                last.then_inc(added, 1)

            def variances(u0, u1):
                for u in range(u0, u1):
                    ins = dve.bn_stats(stats[:, u, :], x_sb[:, u, :])
                link(ins)
                for u in range(u0, u1):
                    ins = dve.bn_aggr(mean_var[:, u, :], stats[:, u, :])
                link(ins)
                dve.tensor_scalar(var_eps[:, u0:u1], mean_var[:, u0:u1, 1], EPS, None, ALU.add
                                  ).then_inc(var_ready, 1)

            def norm1(u0, u1):
                for u in range(u0, u1):
                    dve.tensor_scalar(xn[:, u, :], x_sb[:, u, :], mean_var[:, u, 0:1], rstd[:, u:u + 1],
                                      ALU.subtract, ALU.mult).then_inc(xn_ready, 1)

            dve.wait_ge(x_loaded, 16)
            variances(0, 2)
            dve.wait_ge(rstd_ready, 1)
            norm1(0, 2)
            dve.wait_ge(bias_loaded, 16)
            dve.tensor_scalar(bq_scaled[:, :], bq_all, SCALE, None, ALU.mult).then_inc(bq_ready, 1)
            prep_out(0, LN_T)
            dve.wait_ge(mask_loaded, 16)
            dve.tensor_copy(mask_bf[:, :], mask_sb[:, :]).then_inc(mask_ready, 1)
            dve.wait_ge(bq_ready, 1)
            prep_out(0, Q)
            dve.wait_ge(const_loaded, 16)
            expand0()
            prep_out(0, Q_T)
            heads0(0, GROUPS)
            second_half_rows(1)
            dve.wait_ge(k0_copied, 1)
            prep_out(0, KV)
            heads0(GROUPS, P // ROWS)
            for n in range(BLOCKS):
                maxima(n)
                if n == 0:
                    second_half_rows(2)
                    second_half_rows(3)
                    dve.wait_ge(rest_loaded, 32)
                    variances(2, 4)
                if n == 2:
                    variances(4, TILES)
                if n == PER_BATCH - 2:
                    dve.wait_ge(rstd_ready, 3)
                if n % PER_BATCH == PER_BATCH - 2 and n // PER_BATCH + 2 < B:
                    norm1(2 * (n // PER_BATCH + 2), 2 * (n // PER_BATCH + 3))
                for b, step in PREP_AT[n]:
                    if step < ROWS_0:
                        prep_out(b, step)
                if n == 0:
                    dve.wait_ge(rstd_ready, 2)
                    norm1(2, 4)
                for j, step, u in TILE_AT[n]:
                    if n not in VALUES_AT:
                        tile_out(j, step, u)
                for m in TURN_AT[n]:
                    turned_out(m)
                for j, step, u in TILE_AT[n]:
                    if n in VALUES_AT:
                        tile_out(j, step, u)
                for j, step, u in TILE_AT[n - 1]:
                    if step == GATE and j < B - 2:
                        pick(j)
                if n in FFN_AFTER:
                    b = FFN_AFTER.index(n)
                    for m in TURN_IN_FFN[n]:
                        turned_out(m)
                    add_expert(b, 0)
                    for e in range(1, E):
                        add_expert(b, e)
            b, j = B - 2, B - 1
            pick(B - 2)
            for n in TURN_IN_FFN[BLOCKS - 1]:
                turned_out(n)
            add_expert(b, 0)
            add_expert(b, 1)
            tile_out(j, VALUES_T, TILES - 2)
            add_expert(b, 2)
            tile_out(j, VALUES_T, TILES - 1)
            add_expert(b, 3)
            norm2(j)
            add_expert(b, 4)
            tile_out(j, LN2_T, None)
            add_expert(b, 5)
            tile_out(j, GATE, None)
            add_expert(b, 6)
            add_expert(b, 7)
            pick(j)
            add_expert(b + 1, 0)
            for e in range(1, E):
                add_expert(b + 1, e)


def kernel(x, ctx_1024, L0_xattn_Wq, L0_xattn_bq, L0_xattn_Wk, L0_xattn_bk, L0_xattn_Wv, L0_xattn_bv,
           L0_xattn_Er, L0_ffn_gate, L0_ffn_W1, L0_ffn_b1, L0_ffn_W2, L0_ffn_b2):
    import concourse.bacc as bacc
    from concourse.bass_utils import run_bass_kernel_spmd

    a = lambda v: np.ascontiguousarray(np.asarray(v))
    arrays = {
        "x": a(x),
        "ctxT": a(np.asarray(ctx_1024).reshape(B * S, D).T),
        "wqkv": np.concatenate([np.asarray(L0_xattn_Wq).T, np.asarray(L0_xattn_Wk).T, np.asarray(L0_xattn_Wv).T,
                                np.asarray(L0_xattn_bk).reshape(D, 1)], axis=1),
        "bias": np.concatenate([np.asarray(L0_xattn_bq), np.asarray(L0_xattn_bv)]).reshape(1, 2 * D),
        "er": er_windows(np.asarray(L0_xattn_Er)),
        "gate": a(L0_ffn_gate),
        "w1": a(L0_ffn_W1),
        "b1T": a(np.asarray(L0_ffn_b1).reshape(CHUNKS, P).T),
        "w2": a(L0_ffn_W2),
        "b2": a(L0_ffn_b2).reshape(1, E * D),
    }
    arrays.update(shape_constants())
    nc = bacc.Bacc("TRN2", target_bir_lowering=False, num_devices=1)
    t = {k: nc.dram_tensor("in_" + k, v.shape, mybir.dt.from_np(v.dtype), kind="ExternalInput").ap()
         for k, v in arrays.items()}
    t["out"] = nc.dram_tensor("out", (B, S, D), F32, kind="ExternalOutput").ap()
    build(nc, t)
    r = run_bass_kernel_spmd(nc, [{"in_" + k: v for k, v in arrays.items()}], core_ids=[0])
    return r.results[0]["out"]
```
